# Optimizing a Trainium2 kernel written in Bass

```python
import numpy as np
import jax
import jax.numpy as jnp

def _softmax(x, axis=-1):
    return jax.nn.softmax(x, axis=axis)

def _gelu(x):
    return jax.nn.gelu(x, approximate=True)

def _silu(x):
    return jax.nn.silu(x)

def _sigmoid(x):
    return jax.nn.sigmoid(x)

def _layernorm(x, axis=-1, eps=1e-05):
    m = jnp.mean(x, axis=axis, keepdims=True)
    v = jnp.var(x, axis=axis, keepdims=True)
    return (x - m) / jnp.sqrt(v + eps)

def _scatter_add(tgt, idx, src, axis=0):
    return tgt.at[idx].add(src)

def _segment_sum(src, seg, n):
    return jax.ops.segment_sum(src, seg, n)
kernel_name = 'mk_sandwich_d1_jaxref_r4_c05491'

def setup_inputs(seed: int=0):
    np.random.seed(seed)
    _w = jnp.asarray

    def _L0_attn_setup():
        import jax, jax.numpy as jnp
        import numpy as np
        BATCH = 2
        SEQLEN = 1024
        D_MODEL = 256
        EXPAND = 2
        D_STATE = 128
        HEADDIM = 64
        D_CONV = 4
        NGROUPS = 1
        D_INNER = EXPAND * D_MODEL
        NHEADS = D_INNER // HEADDIM
        CONV_DIM = D_INNER + 2 * NGROUPS * D_STATE
        D_IN_PROJ = 2 * D_INNER + 2 * NGROUPS * D_STATE + NHEADS
        EPS = 1e-05

        def _mamba2_forward(X, W_in, conv_w, conv_b, dt_bias, A_log, D, norm_w, W_out):
            b, l, _ = X.shape
            zxbcdt = jnp.einsum('bld,ed->ble', X, W_in)
            z = zxbcdt[..., :D_INNER]
            xBC = zxbcdt[..., D_INNER:D_INNER + CONV_DIM]
            dt = zxbcdt[..., D_INNER + CONV_DIM:]
            xBC_t = jnp.transpose(xBC, (0, 2, 1))
            conv = jax.lax.conv_general_dilated(xBC_t, conv_w[:, None, :], window_strides=(1,), padding=[(D_CONV - 1, 0)], feature_group_count=CONV_DIM, dimension_numbers=('NCH', 'OIH', 'NCH'))
            xBC = jax.nn.silu(jnp.transpose(conv + conv_b[None, :, None], (0, 2, 1)))
            x = xBC[..., :D_INNER].reshape(b, l, NHEADS, HEADDIM)
            Bm = xBC[..., D_INNER:D_INNER + D_STATE]
            Cm = xBC[..., D_INNER + D_STATE:]
            dt = jax.nn.softplus(dt + dt_bias)
            A = -jnp.exp(A_log)
            dA = jnp.exp(dt * A)

            def step(h, inp):
                dA_t, dtx_t, B_t, C_t = inp
                h = h * dA_t[:, :, None, None] + dtx_t[..., None] * B_t[:, None, None, :]
                y = jnp.einsum('bhpn,bn->bhp', h, C_t)
                return (h, y)
            dtx = dt[..., None] * x
            h0 = jnp.zeros((b, NHEADS, HEADDIM, D_STATE), X.dtype)
            xs = (jnp.transpose(dA, (1, 0, 2)), jnp.transpose(dtx, (1, 0, 2, 3)), jnp.transpose(Bm, (1, 0, 2)), jnp.transpose(Cm, (1, 0, 2)))
            _, ys = jax.lax.scan(step, h0, xs)
            y = jnp.transpose(ys, (1, 0, 2, 3)) + D[None, None, :, None] * x
            y = y.reshape(b, l, D_INNER)
            y = y * jax.nn.silu(z)
            y = y * jax.lax.rsqrt(jnp.mean(jnp.square(y), axis=-1, keepdims=True) + EPS) * norm_w
            return jnp.einsum('ble,de->bld', y, W_out)
        key = jax.random.key(seed)
        ks = jax.random.split(key, 8)
        s = 0.02
        return {'X': jax.random.normal(ks[0], (BATCH, SEQLEN, D_MODEL), jnp.float32), 'W_in': jax.random.normal(ks[1], (D_IN_PROJ, D_MODEL), jnp.float32) * s, 'conv_w': jax.random.normal(ks[2], (CONV_DIM, D_CONV), jnp.float32) * 0.2, 'conv_b': jnp.zeros((CONV_DIM,), jnp.float32), 'dt_bias': jax.random.uniform(ks[3], (NHEADS,), jnp.float32) * 0.1, 'A_log': jnp.log(jax.random.uniform(ks[4], (NHEADS,), jnp.float32, minval=1.0, maxval=16.0)), 'D': jnp.ones((NHEADS,), jnp.float32), 'norm_w': jnp.ones((D_INNER,), jnp.float32), 'W_out': jax.random.normal(ks[5], (D_MODEL, D_INNER), jnp.float32) * s}
    _L0_attn_in = _L0_attn_setup()

    def _L0_ffn_setup():
        import jax, jax.numpy as jnp
        import numpy as np
        TOP_K = 8
        CAPACITY = 128

        def _silu(x):
            return x * jax.nn.sigmoid(x)
        key = jax.random.key(seed)
        ks = jax.random.split(key, 7)
        B, S, H, E, I, Is = (2, 256, 256, 64, 128, 512)
        s = 0.05
        return {'hidden_states': jax.random.normal(ks[0], (B, S, H), jnp.float32), 'gate_w': jax.random.normal(ks[1], (H, E), jnp.float32) * s, 'shared_gate_w': jax.random.normal(ks[2], (H, 1), jnp.float32) * s, 'shared_gate_up_w': jax.random.normal(ks[3], (H, 2 * Is), jnp.float32) * s, 'shared_down_w': jax.random.normal(ks[4], (Is, H), jnp.float32) * s, 'expert_gate_up_w': jax.random.normal(ks[5], (E, H, 2 * I), jnp.float32) * s, 'expert_down_w': jax.random.normal(ks[6], (E, I, H), jnp.float32) * s}
    _L0_ffn_in = _L0_ffn_setup()
    _d = {'L0_attn_X': _L0_attn_in['X'], 'L0_attn_W_in': _L0_attn_in['W_in'], 'L0_attn_conv_w': _L0_attn_in['conv_w'], 'L0_attn_conv_b': _L0_attn_in['conv_b'], 'L0_attn_dt_bias': _L0_attn_in['dt_bias'], 'L0_attn_A_log': _L0_attn_in['A_log'], 'L0_attn_D': _L0_attn_in['D'], 'L0_attn_norm_w': _L0_attn_in['norm_w'], 'L0_attn_W_out': _L0_attn_in['W_out'], 'L0_ffn_gate_w': _L0_ffn_in['gate_w'], 'L0_ffn_shared_gate_w': _L0_ffn_in['shared_gate_w'], 'L0_ffn_shared_gate_up_w': _L0_ffn_in['shared_gate_up_w'], 'L0_ffn_shared_down_w': _L0_ffn_in['shared_down_w'], 'L0_ffn_expert_gate_up_w': _L0_ffn_in['expert_gate_up_w'], 'L0_ffn_expert_down_w': _L0_ffn_in['expert_down_w']}
    _x0 = _d['L0_attn_X']
    _d['L0_attn_X'] = jax.random.normal(jax.random.fold_in(jax.random.key(seed), 1), (2, 4096, 256), dtype=_x0.dtype)
    del _x0
    return _d

def reference(L0_attn_X, L0_attn_W_in, L0_attn_conv_w, L0_attn_conv_b, L0_attn_dt_bias, L0_attn_A_log, L0_attn_D, L0_attn_norm_w, L0_attn_W_out, L0_ffn_gate_w, L0_ffn_shared_gate_w, L0_ffn_shared_gate_up_w, L0_ffn_shared_down_w, L0_ffn_expert_gate_up_w, L0_ffn_expert_down_w):

    def _L0_attn_ref(X, W_in, conv_w, conv_b, dt_bias, A_log, D, norm_w, W_out):
        import jax, jax.numpy as jnp
        import numpy as np
        BATCH = 2
        SEQLEN = 1024
        D_MODEL = 256
        EXPAND = 2
        D_STATE = 128
        HEADDIM = 64
        D_CONV = 4
        NGROUPS = 1
        D_INNER = EXPAND * D_MODEL
        NHEADS = D_INNER // HEADDIM
        CONV_DIM = D_INNER + 2 * NGROUPS * D_STATE
        D_IN_PROJ = 2 * D_INNER + 2 * NGROUPS * D_STATE + NHEADS
        EPS = 1e-05

        def _mamba2_forward(X, W_in, conv_w, conv_b, dt_bias, A_log, D, norm_w, W_out):
            b, l, _ = X.shape
            zxbcdt = jnp.einsum('bld,ed->ble', X, W_in)
            z = zxbcdt[..., :D_INNER]
            xBC = zxbcdt[..., D_INNER:D_INNER + CONV_DIM]
            dt = zxbcdt[..., D_INNER + CONV_DIM:]
            xBC_t = jnp.transpose(xBC, (0, 2, 1))
            conv = jax.lax.conv_general_dilated(xBC_t, conv_w[:, None, :], window_strides=(1,), padding=[(D_CONV - 1, 0)], feature_group_count=CONV_DIM, dimension_numbers=('NCH', 'OIH', 'NCH'))
            xBC = jax.nn.silu(jnp.transpose(conv + conv_b[None, :, None], (0, 2, 1)))
            x = xBC[..., :D_INNER].reshape(b, l, NHEADS, HEADDIM)
            Bm = xBC[..., D_INNER:D_INNER + D_STATE]
            Cm = xBC[..., D_INNER + D_STATE:]
            dt = jax.nn.softplus(dt + dt_bias)
            A = -jnp.exp(A_log)
            dA = jnp.exp(dt * A)

            def step(h, inp):
                dA_t, dtx_t, B_t, C_t = inp
                h = h * dA_t[:, :, None, None] + dtx_t[..., None] * B_t[:, None, None, :]
                y = jnp.einsum('bhpn,bn->bhp', h, C_t)
                return (h, y)
            dtx = dt[..., None] * x
            h0 = jnp.zeros((b, NHEADS, HEADDIM, D_STATE), X.dtype)
            xs = (jnp.transpose(dA, (1, 0, 2)), jnp.transpose(dtx, (1, 0, 2, 3)), jnp.transpose(Bm, (1, 0, 2)), jnp.transpose(Cm, (1, 0, 2)))
            _, ys = jax.lax.scan(step, h0, xs)
            y = jnp.transpose(ys, (1, 0, 2, 3)) + D[None, None, :, None] * x
            y = y.reshape(b, l, D_INNER)
            y = y * jax.nn.silu(z)
            y = y * jax.lax.rsqrt(jnp.mean(jnp.square(y), axis=-1, keepdims=True) + EPS) * norm_w
            return jnp.einsum('ble,de->bld', y, W_out)
        return _mamba2_forward(X, W_in, conv_w, conv_b, dt_bias, A_log, D, norm_w, W_out)

    def _L0_ffn_ref(hidden_states, gate_w, shared_gate_w, shared_gate_up_w, shared_down_w, expert_gate_up_w, expert_down_w):
        import jax, jax.numpy as jnp
        import numpy as np
        TOP_K = 8
        CAPACITY = 128

        def _silu(x):
            return x * jax.nn.sigmoid(x)
        B, S, H = hidden_states.shape
        x = hidden_states.reshape(-1, H)
        T = x.shape[0]
        E = gate_w.shape[1]
        Is = shared_gate_up_w.shape[1] // 2
        I = expert_gate_up_w.shape[2] // 2
        gu = x @ shared_gate_up_w
        shared = _silu(gu[:, :Is]) * gu[:, Is:] @ shared_down_w
        shared = shared * jax.nn.sigmoid(x @ shared_gate_w)
        logits = x @ gate_w
        probs = jax.nn.softmax(logits.astype(jnp.float32), axis=-1)
        w, idx = jax.lax.top_k(probs, TOP_K)
        w = (w / jnp.sum(w, axis=-1, keepdims=True)).astype(x.dtype)
        e_flat = idx.reshape(-1)
        w_flat = w.reshape(-1)
        A = e_flat.shape[0]
        tok = jnp.arange(A) // TOP_K
        onehot = jax.nn.one_hot(e_flat, E, dtype=jnp.int32)
        pos = jnp.take_along_axis(jnp.cumsum(onehot, axis=0) - 1, e_flat[:, None], axis=1)[:, 0]
        slot = jnp.minimum(pos, CAPACITY)
        buf = jnp.zeros((E, CAPACITY + 1, H), x.dtype).at[e_flat, slot].set(x[tok])
        gu_e = jnp.einsum('ech,ehf->ecf', buf, expert_gate_up_w)
        act = _silu(gu_e[..., :I]) * gu_e[..., I:]
        out_e = jnp.einsum('eci,eih->ech', act, expert_down_w)
        y = out_e[e_flat, slot] * w_flat[:, None]
        y = jnp.where((pos < CAPACITY)[:, None], y, jnp.zeros_like(y))
        y = y.reshape(T, TOP_K, H).sum(axis=1)
        return (y + shared).reshape(B, S, H)
    x = L0_attn_X
    x = x + _layernorm(_L0_attn_ref(_layernorm(x, axis=-1), L0_attn_W_in, L0_attn_conv_w, L0_attn_conv_b, L0_attn_dt_bias, L0_attn_A_log, L0_attn_D, L0_attn_norm_w, L0_attn_W_out), axis=-1)
    x = x + _layernorm(_L0_ffn_ref(_layernorm(x, axis=-1), L0_ffn_gate_w, L0_ffn_shared_gate_w, L0_ffn_shared_gate_up_w, L0_ffn_shared_down_w, L0_ffn_expert_gate_up_w, L0_ffn_expert_down_w), axis=-1)
    return x

_drawn_inputs = setup_inputs


def setup_inputs(seed=0):
    import zlib

    import numpy as np

    out = dict(_drawn_inputs(seed))
    spreads = {'L0_attn_conv_b': (0.0, 0.1), 'L0_attn_D': (1.0, 0.2), 'L0_attn_norm_w': (1.0, 0.2)}
    factors = {'L0_attn_dt_bias': 35.013, 'L0_attn_A_log': 6.115}
    for name, (base, spread) in spreads.items():
        noise = np.random.default_rng([zlib.crc32(name.encode()), seed]).standard_normal(out[name].shape)
        drawn = base * np.exp(spread * noise) if base else spread * noise
        out[name] = jnp.asarray(drawn.astype(out[name].dtype))
    for name, factor in factors.items():
        out[name] = (out[name] * factor).astype(out[name].dtype)
    return out
```

```python
import numpy as np
import concourse.bass as bass
from concourse import mybir
from concourse.alu_op_type import AluOpType as ALU
from contextlib import ExitStack

F32 = mybir.dt.float32
F32R = mybir.dt.float32r
BF16 = mybir.dt.bfloat16
U32 = mybir.dt.uint32
ACT = mybir.ActivationFunctionType
AX = mybir.AxisListType

P = 128
NB, LEN, DM = 2, 4096, 256
STEPS = LEN // P
TILES = NB * STEPS
TOK = NB * LEN
KD = DM // P
DI, NH, HD, NS = 512, 8, 64, 128
CONV = DI + 2 * NS
CT = CONV // P
TAPS = 4
HALO = TAPS - 1
KI = DI // P
EPS = 1e-5
NE, TOPK, CAP = 64, 8, 128
FI, FS = 128, 512
ROW = DM + NE
NEVER = -3.0e38


class Steps:

    def __init__(self, i, inner=False):
        def at(d):
            return i + d if inner or 0 <= i + d < STEPS else None
        self.cur, self.prev, self.prev2 = at(0), at(-1), at(-2)
        self.nxt, self.nxt2, self.far = at(1), at(2), at(5)


def is_number(j):
    return isinstance(j, int)


def plain(v):
    return v.bitcast(F32)


def follows(step):
    return not is_number(step) or step > 0


def pipeline(eng, iteration):
    first, last = 2, STEPS - 5
    for i in range(-2, first):
        iteration(Steps(i))
    with eng.Fori(first, last) as i:
        iteration(Steps(i, inner=True))
    for i in range(last, STEPS + 2):
        iteration(Steps(i))


def build(nc, x_d, w_in_d, conv_w_d, conv_b_d, dt_bias_d, a_log_d, d_d, norm_w_d, w_out_d,
          gate_d, sgate_d, sgu_d, sdown_d, egu_d, edown_d, out_d):
    tokens_d = nc.dram_tensor("token_table", (TOK + CAP, ROW), F32, kind="Internal").ap()
    routed_d = nc.dram_tensor("routed_sum", (TOK + CAP, DM), F32, kind="Internal").ap()
    counts_d = nc.dram_tensor("count_table", ((TILES + 1) * NE, P), F32, kind="Internal").ap()
    ends_d = nc.dram_tensor("count_ends", (NE, TILES), F32, kind="Internal").ap()
    xnt_d = nc.dram_tensor("normed_transposed", (STEPS, P, KD * NB * P), F32, kind="Internal").ap()

    ctx = ExitStack()
    with ctx:
        def sb(name, shape, dt=F32):
            return ctx.enter_context(nc.sbuf_tensor(name, shape, dt))

        phase = []

        def sem(name):
            if not phase:
                phase.append(ExitStack())
            phase.append(phase[0].enter_context(nc.semaphore(name)))
            return phase[-1]

        def end_phase():
            numbers = sorted(s.num for s in phase[1:])
            starts = [n for n in numbers if n - 1 not in numbers]
            with nc.Block() as block:
                @block.sync
                def _(eng):
                    for n in starts:
                        end = n
                        while end in numbers:
                            end += 1
                        eng.sem_clear(range(n, end))
            phase.pop(0).close()
            phase.clear()

        def sems(name, n=2):
            return [sem(f"{name}{k}") for k in range(n)]

        x_all = sb("x_all", [P, NB, STEPS, DM])
        counts = sb("counts", [P, STEPS * P])
        shared_tanh = sb("shared_tanh", [P, NB, STEPS])
        identity = sb("identity", [P, P])
        upto = sb("upto", [P, P])
        beyond = sb("beyond", [P, P])
        ones = sb("ones", [P, P])
        upto_bf = sb("upto_bf", [P, P], BF16)
        count_now = sb("count_now", [P, 1])
        minus_half = sb("minus_half", [P, NB])
        bank_m = ctx.enter_context(nc.psum_tensor("bank_m", [P, 512], F32))
        bank_w = ctx.enter_context(nc.psum_tensor("bank_w", [P, 512], F32))
        bank_ty = ctx.enter_context(nc.psum_tensor("bank_ty", [P, NB, 512], F32))
        bank_p = ctx.enter_context(nc.psum_tensor("bank_p", [P, NB, 512], F32))
        bank_s = ctx.enter_context(nc.psum_tensor("bank_s", [P, 2, 512], F32))

        memory = ExitStack()
        arena = [memory.enter_context(nc.sbuf_tensor("mamba_arena", [P, 27000], F32)), 0]

        def view(*shape):
            n = int(np.prod(shape))
            v = arena[0][:, arena[1]:arena[1] + n]
            arena[1] += n
            assert arena[1] <= arena[0].shape[1], arena[1]
            names = "abcd"[:len(shape)]
            if len(shape) > 1:
                v = v.rearrange(f"p ({' '.join(names)}) -> p {' '.join(names)}",
                                **{k: s for k, s in zip(names[1:], shape[1:])})
            return v

        w_in = view(KD, 2 * DI + 2 * NS + NH)
        w_out = view(KI, DM)
        w_gate = view(KD, NE + 1)
        w_sgate = view(KD)
        conv_w = view(CT, TAPS)
        conv_b = view(CT, 1)
        norm_w = view(KI, 1)
        dt_bias = view(NB, NH)
        a_neg = view(NB, NH)
        d_skip = view(NH)
        raw = view(CT, NB, HALO + P)
        half = view(CT, NB, P)
        tanh_x = view(CT, NB, P)
        xbc = view(CT, NB, P)
        x_norm = view(NB, DM)
        xnt = view(KD, NB, P)
        tanh_z = view(NB, DI)
        gate_z = view(NB, DI)
        seg_in = view(NB, NH, P)
        decay = view(NB, NH, P)
        cb = view(NB, P)
        b_tok = view(NB, NS)
        x_tok = view(NB, NH, HD)
        xdt = view(NB, NH, HD)
        xw = view(NB, NH, HD)
        y = view(NB, NH, HD)
        yt = view(NB, KI, P)
        state = view(NB, NH, HD)
        o_norm = view(NB, DM)
        x2_norm = view(NB, DM)
        x2t = view(KD, NB, P)
        weights = view(NB, NE)
        squares = view(DI)
        decays = view(3, NB, NH)
        st_x, st_o, st_2 = view(NB, 6), view(NB, 6), view(NB, 6)
        mv_x, mv_o, mv_2 = view(NB, 2), view(NB, 2), view(NB, 2)
        ve_x, ve_o, ve_2 = view(NB), view(NB), view(NB)
        rs_x, rs_o, rs_2 = view(NB), view(NB), view(NB)
        shift_o, square_sum, eps_o = view(NB), view(NB), view(NB)
        sp = {k: view(NB, NH) for k in ("x", "nabs", "u", "w", "d", "ln", "num", "den", "q", "inv", "sp", "dt", "a")}
        logit = view(NB, NE + 1)
        top8 = view(NB, TOPK)
        neg_max = view(NB)
        expd = view(NB, NE)
        rest = view(NB, NE)
        picked = view(NB, NE)
        top_sum = view(NB)
        top_inv = view(NB)
        chosen = memory.enter_context(nc.sbuf_tensor("chosen", [P, NB, NE], BF16))
        zeros = tanh_x[:, 0:4, :, :].rearrange("p c b t -> p (c b t)")

        s_mem = sem("s_mem")
        s_sel = sem("s_sel")
        s_wload = sem("s_wload")
        s_wraw = sem("s_wraw")
        s_zero = sem("s_zero")
        s_fill = sem("s_fill")
        s_alog = sem("s_alog")
        s_prep = sem("s_prep")

        with nc.Block() as block:
            @block.gpsimd
            def _(pool):
                for m, v in ((identity, 0.0), (upto, 1.0), (beyond, 1.0), (ones, 1.0), (minus_half, -0.5)):
                    nc.gpsimd.memset(m[:, :], v).then_inc(s_mem, 1)
                pool.wait_ge(s_mem, 5)
                nc.gpsimd.affine_select(out=identity[:, :], in_=identity[:, :], compare_op=ALU.not_equal,
                                        fill=1.0, base=0, pattern=[[-1, P]], channel_multiplier=1).then_inc(s_sel, 1)
                nc.gpsimd.affine_select(out=upto[:, :], in_=upto[:, :], compare_op=ALU.is_ge,
                                        fill=0.0, base=0, pattern=[[1, P]], channel_multiplier=-1).then_inc(s_sel, 1)
                nc.gpsimd.affine_select(out=beyond[:, :], in_=beyond[:, :], compare_op=ALU.is_gt,
                                        fill=0.0, base=0, pattern=[[-1, P]], channel_multiplier=1).then_inc(s_sel, 1)

            @block.vector
            def _(dve):
                nc.vector.memset(zeros, 0.0).then_inc(s_zero, 1)
                nc.vector.memset(raw[:, :, :, 0:HALO], 0.0)
                nc.vector.memset(state, 0.0)
                nc.vector.memset(count_now[:, :], 0.0)
                dve.wait_ge(s_sel, 3)
                nc.vector.tensor_copy(upto_bf[:, :], upto[:, :])
                dve.wait_ge(s_wraw, 16 * 8)
                nc.vector.tensor_copy(w_gate[:, :, NE], w_sgate)
                for k in range(KI):
                    nc.vector.tensor_scalar(w_out[:, k, :], w_out[:, k, :], norm_w[:, k, :], None, ALU.mult)
                nc.vector.tensor_scalar(conv_w, conv_w, 0.5, None, ALU.mult)
                nc.vector.tensor_scalar(conv_b, conv_b, 0.5, None, ALU.mult)
                dve.wait_ge(s_alog, 1)
                nc.vector.tensor_scalar(a_neg, a_neg, -1.0, None, ALU.mult).then_inc(s_prep, 1)

            @block.scalar
            def _(act):
                act.wait_ge(s_wraw, 16 * 8)
                nc.scalar.activation(a_neg, a_neg, ACT.Exp).then_inc(s_alog, 1)
                act.wait_ge(s_wload, 16 * 4)

            @block.sync
            def _(sp_):
                def spread(v, n):
                    return v.rearrange("(a n) -> a n", a=1).partition_broadcast(P)
                sp_.dma_start(w_out, w_out_d.rearrange("(k p) m -> p k m", p=P)).then_inc(s_wraw, 16)
                sp_.dma_start(norm_w, norm_w_d.rearrange("p (k one) -> p k one", one=1)).then_inc(s_wraw, 16)
                sp_.dma_start(conv_w, conv_w_d).then_inc(s_wraw, 16)
                sp_.dma_start(conv_b, conv_b_d.rearrange("p (c one) -> p c one", one=1)).then_inc(s_wraw, 16)
                for b in range(NB):
                    sp_.dma_start(a_neg[:, b, :], a_log_d.partition_broadcast(P)).then_inc(s_wraw, 16)
                    sp_.dma_start(dt_bias[:, b, :], dt_bias_d.partition_broadcast(P)).then_inc(s_wload, 16)
                sp_.dma_start(d_skip, d_d.partition_broadcast(P)).then_inc(s_wraw, 16)
                sp_.dma_start(w_in, w_in_d.rearrange("(k p) e -> p k e", p=P)).then_inc(s_wload, 16)
                sp_.dma_start(w_gate[:, :, 0:NE], gate_d.rearrange("(k p) e -> p k e", p=P)).then_inc(s_wload, 16)
                sp_.dma_start(w_sgate, sgate_d).then_inc(s_wraw, 16)
                sp_.wait_ge(s_zero, 1)
                sp_.dma_start(routed_d.rearrange("(p a) d -> p (a d)", p=P)[:, 0:16 * 1024]
                              .rearrange("p (a f) -> p a f", f=1024),
                              zeros.rearrange("p (one f) -> p one f", one=1).broadcast_to([P, 16, 1024])).then_inc(s_fill, 16)
                sp_.dma_start(routed_d.rearrange("(p a) d -> p (a d)", p=P)[:, 16 * 1024:],
                              zeros[:, 0:256]).then_inc(s_fill, 16)
                sp_.dma_start(tokens_d[TOK:TOK + CAP, :], zeros[:, 0:ROW]).then_inc(s_fill, 16)
                sp_.wait_ge(s_fill, 16 * 3)

        def of_step(t, j):
            if is_number(j):
                return t[:, :, j]
            if len(t.shape) == 3:
                return t[:, :, bass.ds(j, 1)].rearrange("p b o -> p (b o)")
            return t[:, :, bass.ds(j, 1), :].rearrange("p b o d -> p b (o d)")

        end_phase()

        x_loaded = sem("x_loaded")
        x_norm_ready, xnt_turned, xnt_ready = sem("x_norm_ready"), sem("xnt_turned"), sem("xnt_ready")
        xbc_projected, raw_ready, halo_kept = sems("xbc_projected", 3), sems("raw_ready", 3), sem("halo_kept")
        tap_ready, conv_ready, tanh_x_ready = sems("tap_ready", 3), sems("conv_ready", 2), sems("tanh_x_ready", 2)
        conv_link = sem("conv_link")
        xbc_ready = sem("xbc_ready")
        z_projected, tanh_z_ready, gate_z_ready = sems("z_projected", 2), sems("tanh_z_ready", 2), sems("gate_z_ready", 2)
        dt_projected, dt_taken, dt_exp, dt_ln = sem("dt_projected"), sem("dt_taken"), sem("dt_exp"), sem("dt_ln")
        softplus = sem("softplus")
        a_ready = sem("a_ready")
        sums_done, decays_ready = sem("sums_done"), sem("decays_ready")
        cb_done, cb_ready, b_tok_ready = sem("cb_done"), sem("cb_ready"), sem("b_tok_ready")
        seg_in_ready, seg_done, exp_ready, mix_ready = sems("seg_in_ready", 2), sems("seg_done", 2), sems("exp_ready", 2), sems("mix_ready", 2)
        x_turned, x_tok_ready, xdt_ready, xw_ready = sems("x_turned", 2), sems("x_tok_ready", 2), sems("xdt_ready", 2), sems("xw_ready", 2)
        skip_ready = sems("skip_ready", 2)
        read_done, state_decayed, update_done, state_ready = sems("read_done", 2), sems("state_decayed", 2), sems("update_done", 2), sems("state_ready", 2)
        inter_ready, inter_skip, intra_done, y_sum, y_ready = sems("inter_ready", 2), sems("inter_skip", 2), sems("intra_done", 2), sems("y_sum", 2), sems("y_ready", 2)
        y_turned, yt_ready, squares_ready = sems("y_turned", 2), sems("yt_ready", 2), sems("squares_ready", 2)
        o_done, o_link, o_power, o_scale, o_applied, x2_ready = sem("o_done"), sem("o_link"), sem("o_power"), sem("o_scale"), sem("o_applied"), sem("x2_ready")
        ln1_link, ln1_power = sem("ln1_link"), sem("ln1_power")
        ln2_link, ln2_power, x2_norm_ready = sem("ln2_link"), sem("ln2_power"), sem("x2_norm_ready")
        x2_turned, x2t_ready = sem("x2_turned"), sem("x2t_ready")
        logits_done, logit_ready, max_ready, expd_ready = sem("logits_done"), sem("logit_ready"), sem("max_ready"), sem("expd_ready")
        route_link, chosen_ready, weights_ready = sem("route_link"), sem("chosen_ready"), sem("weights_ready")
        counts_done, counts_ready, count_kept, tanh_s_done = sem("counts_done"), sem("counts_ready"), sem("count_kept"), sem("tanh_s_done")
        stored_rows, stored_xnt, stored_weights = sem("stored_rows"), sem("stored_xnt"), sem("stored_weights")

        LN, SOFT, ROUTE, TAP = 3, 7, 5, 4

        with nc.Block() as block:
            @block.sync
            def _(eng):
                def load(j):
                    eng.dma_start(of_step(x_all, j),
                                  x_d[:, bass.ds(j * P, P), :].rearrange("b p d -> p b d")).then_inc(x_loaded, 16)

                for j in range(3):
                    load(j)
                    eng.wait_ge(x_loaded, 16 * (j + 1))

                def iteration(s):
                    if s.far is not None:
                        load(s.far)
                        eng.wait_ge(x_loaded, 16 * s.far + 16)
                    if s.prev is not None:
                        eng.wait_ge(x2_norm_ready, s.prev + 1)
                        for b in range(NB):
                            eng.dma_start(tokens_d[bass.ds(s.prev * P + b * LEN, P), 0:DM],
                                          x2_norm[:, b, :]).then_inc(stored_rows, 16)
                        eng.wait_ge(x2t_ready, s.prev + 1)
                        eng.dma_start(xnt_d[bass.ds(s.prev, 1), :, :].rearrange("o p f -> (o p) f"),
                                      x2t.rearrange("p k b t -> p (k b t)")).then_inc(stored_xnt, 16)
                    if s.prev2 is not None:
                        eng.wait_ge(weights_ready, s.prev2 + 1)
                        for b in range(NB):
                            eng.dma_start(tokens_d[bass.ds(s.prev2 * P + b * LEN, P), DM:ROW],
                                          weights[:, b, :]).then_inc(stored_weights, 16)
                pipeline(eng, iteration)
                eng.wait_ge(stored_rows, 32 * STEPS)
                eng.wait_ge(stored_xnt, 16 * STEPS)
                eng.wait_ge(stored_weights, 32 * STEPS)

            @block.tensor
            def _(eng):
                def transpose(out, in_):
                    return nc.tensor.transpose(out, in_, identity[:, :])

                def seg(s, b):
                    eng.wait_ge(seg_in_ready[b], s.cur + 1)
                    for q in range(2):
                        last = nc.tensor.matmul(bank_s[:, q, :], beyond[:, :],
                                                seg_in[:, b, 4 * q:4 * q + 4, :].rearrange("p h t -> p (h t)"),
                                                start=True, stop=True)
                    last.then_inc(seg_done[b], 1)

                def iteration(s):
                    if s.cur is not None:
                        eng.wait_ge(raw_ready[2], s.cur + 1)
                        seg(s, 0)
                        eng.wait_ge(xbc_ready, s.cur + 1)
                        for b in range(NB):
                            eng.wait_ge(gate_z_ready[b], s.cur + 1)
                            for c in range(KI):
                                last = transpose(bank_p[:, b, c * P:(c + 1) * P], xbc[:, c, b, :])
                            last.then_inc(x_turned[b], 1)
                        eng.wait_ge(a_ready, s.cur + 1)
                        if s.nxt is not None:
                            eng.wait_ge(xnt_ready, s.nxt + 1)
                        else:
                            if follows(s.cur):
                                eng.wait_ge(inter_ready[1], s.cur)
                        a2 = sp["a"].rearrange("p b h -> p (b h)")
                        for q, mask in enumerate((upto, beyond, ones)):
                            nc.tensor.matmul(bank_m[:, 256 + q * NB * NH:256 + (q + 1) * NB * NH], mask[:, :], a2,
                                             start=True, stop=True)
                        for b in range(NB):
                            last = nc.tensor.matmul(bank_m[:, b * P:(b + 1) * P], xbc[:, 4, b, :], xbc[:, 5, b, :],
                                                    start=True, stop=True)
                        last.then_inc(cb_done, 1)
                        if s.prev2 is not None:
                            eng.wait_ge(x2t_ready, s.prev2 + 1)
                        else:
                            if follows(s.cur):
                                eng.wait_ge(inter_ready[0], s.cur)
                            eng.wait_ge(dt_taken, s.cur + 1)
                        for b in range(NB):
                            last = transpose(bank_w[:, 256 + b * P:256 + (b + 1) * P], xbc[:, 4, b, :])
                        last.then_inc(sums_done, 1)
                    if s.prev2 is not None:
                        eng.wait_ge(x2t_ready, s.prev2 + 1)
                        for b in range(NB):
                            for k in range(KD):
                                last = nc.tensor.matmul(bank_w[:, b * (NE + 1):(b + 1) * (NE + 1)], x2t[:, k, b, :],
                                                        w_gate[:, k, :], start=k == 0, stop=k == KD - 1)
                        last.then_inc(logits_done, 1)
                    if s.cur is not None:
                        eng.wait_ge(exp_ready[0], s.cur + 1)
                        seg(s, 1)
                    if s.prev is not None:
                        for b in range(NB):
                            eng.wait_ge(y_ready[b], s.prev + 1)
                            for c in range(KI):
                                last = transpose(bank_ty[:, b, c * P:(c + 1) * P],
                                                 y[:, b].rearrange("p h d -> p (h d)")[:, c * P:(c + 1) * P])
                            last.then_inc(y_turned[b], 1)
                    if s.prev2 is not None:
                        eng.wait_ge(chosen_ready, s.prev2 + 1)
                        if s.cur is not None:
                            eng.wait_ge(b_tok_ready, s.cur + 1)
                        for b in range(NB):
                            last = nc.tensor.matmul(bank_w[b * NE:(b + 1) * NE, 0:P], chosen[:, b, :], upto_bf[:, :],
                                                    start=True, stop=True)
                        last.then_inc(counts_done, 1)
                    if s.nxt is not None:
                        eng.wait_ge(xnt_ready, s.nxt + 1)
                        if s.cur is not None:
                            eng.wait_ge(b_tok_ready, s.cur + 1)
                        for b in range(NB):
                            for k in range(KD):
                                last = nc.tensor.matmul(bank_w[:, 256 + b * NH:256 + (b + 1) * NH], xnt[:, k, b, :],
                                                        w_in[:, k, DI + CONV:], start=k == 0, stop=k == KD - 1)
                        last.then_inc(dt_projected, 1)
                    if s.prev is not None:
                        eng.wait_ge(yt_ready[0], s.prev + 1)
                        eng.wait_ge(yt_ready[1], s.prev + 1)
                        for b in range(NB):
                            for c in range(KI):
                                last = nc.tensor.matmul(bank_ty[:, 0, b * DM:(b + 1) * DM], yt[:, b, c, :], w_out[:, c, :],
                                                        start=c == 0, stop=c == KI - 1)
                        last.then_inc(o_done, 1)
                    if s.nxt is not None:
                        for g in range(3):
                            if s.cur is not None:
                                eng.wait_ge(cb_ready if g == 0 else exp_ready[1], s.cur + 1)
                            bank = bank_m[:, :] if g == 0 else bank_s[:, g - 1, :]
                            for c in (2 * g, 2 * g + 1):
                                for k in range(KD):
                                    last = nc.tensor.matmul(bank[:, (c % 2) * 256:(c % 2) * 256 + 256],
                                                            w_in[:, k, DI + c * P:DI + (c + 1) * P],
                                                            xnt[:, k].rearrange("p b t -> p (b t)"),
                                                            start=k == 0, stop=k == KD - 1)
                            last.then_inc(xbc_projected[g], 1)
                    if s.cur is not None:
                        for b in range(NB):
                            if b == 0:
                                if s.prev2 is not None:
                                    eng.wait_ge(counts_ready, s.prev2 + 1)
                                if s.nxt is not None:
                                    eng.wait_ge(dt_taken, s.nxt + 1)
                                eng.wait_ge(b_tok_ready, s.cur + 1)
                            elif s.nxt is not None:
                                eng.wait_ge(raw_ready[0], s.nxt + 1)
                            else:
                                eng.wait_ge(cb_ready, s.cur + 1)
                            if follows(s.cur):
                                eng.wait_ge(state_ready[b], s.cur)
                            bank = bank_m if b else bank_w
                            nc.tensor.matmul(bank[:, :], xbc[:, 5, b, :], state[:, b].rearrange("p h d -> p (h d)"),
                                             start=True, stop=True).then_inc(read_done[b], 1)
                        eng.wait_ge(b_tok_ready, s.cur + 1)
                        for b in range(NB):
                            eng.wait_ge(x_tok_ready[b], s.cur + 1)
                            eng.wait_ge(xw_ready[b], s.cur + 1)
                            nc.tensor.matmul(bank_p[:, b, :], b_tok[:, b, :], xw[:, b].rearrange("p h d -> p (h d)"),
                                             start=True, stop=True).then_inc(update_done[b], 1)
                        for b in range(NB):
                            if s.prev is not None:
                                eng.wait_ge(o_applied if b == 0 else yt_ready[1], s.prev + 1)
                            eng.wait_ge(xdt_ready[b], s.cur + 1)
                            eng.wait_ge(mix_ready[b], s.cur + 1)
                            for h in range(NH):
                                last = nc.tensor.matmul(bank_ty[:, b, h * HD:(h + 1) * HD], decay[:, b, h, :],
                                                        xdt[:, b, h, :], start=True, stop=True)
                            last.then_inc(intra_done[b], 1)
                    if s.nxt is not None:
                        for b in range(NB):
                            if s.cur is not None:
                                eng.wait_ge(state_ready[b], s.cur + 1)
                            for k in range(KD):
                                last = nc.tensor.matmul(bank_p[:, b, :], xnt[:, k, b, :], w_in[:, k, 0:DI],
                                                        start=k == 0, stop=k == KD - 1)
                            last.then_inc(z_projected[b], 1)
                    if s.prev is not None:
                        if s.cur is not None:
                            eng.wait_ge(inter_ready[0], s.cur + 1)
                        elif s.prev2 is not None:
                            eng.wait_ge(counts_ready, s.prev2 + 1)
                        eng.wait_ge(x2_norm_ready, s.prev + 1)
                        for b in range(NB):
                            for k in range(KD):
                                last = transpose(bank_w[:, (k * NB + b) * P:(k * NB + b + 1) * P],
                                                 x2_norm[:, b, k * P:(k + 1) * P])
                        last.then_inc(x2_turned, 1)
                    if s.nxt2 is not None:
                        if s.cur is not None:
                            eng.wait_ge(inter_ready[1], s.cur + 1)
                        elif s.nxt is not None:
                            eng.wait_ge(raw_ready[0], s.nxt + 1)
                        eng.wait_ge(x_norm_ready, s.nxt2 + 1)
                        for b in range(NB):
                            for k in range(KD):
                                last = transpose(bank_m[:, (k * NB + b) * P:(k * NB + b + 1) * P],
                                                 x_norm[:, b, k * P:(k + 1) * P])
                        last.then_inc(xnt_turned, 1)
                pipeline(eng, iteration)

            @block.scalar
            def _(eng):
                def flat(v):
                    return v.rearrange("p h d -> p (h d)")

                def copy(out, in_):
                    return nc.scalar.activation(out, in_, ACT.Copy)

                def take_raw(s, g):
                    eng.wait_ge(xbc_projected[g], s.nxt + 1)
                    if g == 0:
                        if follows(s.nxt):
                            eng.wait_ge(halo_kept, s.nxt)
                        if follows(s.nxt):
                            eng.wait_ge(xbc_ready, s.nxt)
                    bank = bank_m[:, :] if g == 0 else bank_s[:, g - 1, :]
                    copy(raw[:, 2 * g:2 * g + 2, :, HALO:], bank.rearrange("p (c b t) -> p c b t", c=2, b=NB)
                         ).then_inc(raw_ready[g], 1)
                    eng.wait_ge(raw_ready[g], s.nxt + 1)
                    for c in (2 * g, 2 * g + 1):
                        last = nc.scalar.activation(half[:, c], raw[:, c, :, HALO:], ACT.Identity,
                                                    bias=conv_b[:, c, :], scale=conv_w[:, c, TAPS - 1:TAPS])
                    last.then_inc(tap_ready[g], 1)

                def iteration(s):
                    if s.cur is not None:
                        for b in range(NB):
                            eng.wait_ge(x_turned[b], s.cur + 1)
                            if follows(s.cur):
                                eng.wait_ge(inter_skip[b], s.cur)
                            copy(flat(x_tok[:, b]), bank_p[:, b, :]).then_inc(x_tok_ready[b], 1)
                            if b == 0:
                                eng.wait_ge(seg_done[0], s.cur + 1)
                                if follows(s.cur):
                                    eng.wait_ge(intra_done[0], s.cur)
                                nc.scalar.activation(flat(decay[:, 0]), bank_s[:, :, :].rearrange("p q f -> p (q f)"),
                                                     ACT.Exp).then_inc(exp_ready[0], 1)
                        eng.wait_ge(cb_done, s.cur + 1)
                        if follows(s.cur):
                            eng.wait_ge(inter_ready[1], s.cur)
                        if follows(s.cur):
                            eng.wait_ge(state_decayed[1], s.cur)
                        if follows(s.cur):
                            eng.wait_ge(xw_ready[1], s.cur)
                        nc.scalar.activation(decays.rearrange("p q b h -> p (q b h)"), bank_m[:, 256:256 + 3 * NB * NH],
                                             ACT.Exp).then_inc(decays_ready, 1)
                        eng.wait_ge(sums_done, s.cur + 1)
                        if s.prev2 is not None:
                            eng.wait_ge(logits_done, s.prev2 + 1)
                        if follows(s.cur):
                            eng.wait_ge(update_done[1], s.cur)
                        copy(b_tok.rearrange("p b n -> p (b n)"), bank_w[:, 256:512]).then_inc(b_tok_ready, 1)
                        eng.wait_ge(seg_done[1], s.cur + 1)
                        if follows(s.cur):
                            eng.wait_ge(intra_done[1], s.cur)
                        nc.scalar.activation(flat(decay[:, 1]), bank_s[:, :, :].rearrange("p q f -> p (q f)"),
                                             ACT.Exp).then_inc(exp_ready[1], 1)
                    if s.prev is not None:
                        for b in range(NB):
                            eng.wait_ge(y_ready[b], s.prev + 1)
                            if b == 0:
                                if follows(s.prev):
                                    eng.wait_ge(o_link, LN * s.prev)
                                if follows(s.prev):
                                    eng.wait_ge(o_done, s.prev)
                            else:
                                eng.wait_ge(squares_ready[0], s.prev + 1)
                            nc.scalar.activation(squares, flat(y[:, b]), ACT.Square,
                                                 accum_out=square_sum[:, b:b + 1]).then_inc(squares_ready[b], 1)
                            eng.wait_ge(y_turned[b], s.prev + 1)
                            copy(yt[:, b].rearrange("p c t -> p (c t)"), bank_ty[:, b, :]).then_inc(yt_ready[b], 1)
                    if s.prev2 is not None:
                        eng.wait_ge(max_ready, s.prev2 + 1)
                        if follows(s.prev2):
                            eng.wait_ge(route_link, ROUTE * s.prev2)
                        for b in range(NB):
                            last = nc.scalar.activation(expd[:, b, :], logit[:, b, 0:NE], ACT.Exp,
                                                        bias=neg_max[:, b:b + 1])
                        last.then_inc(expd_ready, 1)
                        nc.scalar.activation(of_step(shared_tanh, s.prev2), logit[:, :, NE], ACT.Tanh,
                                             scale=0.5).then_inc(tanh_s_done, 1)
                    if s.nxt is not None:
                        eng.wait_ge(softplus, SOFT * s.nxt + 1)
                        if follows(s.nxt):
                            eng.wait_ge(a_ready, s.nxt)
                        nc.scalar.activation(sp["u"], sp["nabs"], ACT.Exp).then_inc(dt_exp, 1)
                        take_raw(s, 0)
                        eng.wait_ge(softplus, SOFT * s.nxt + 2)
                        nc.scalar.activation(sp["ln"], sp["w"], ACT.Ln).then_inc(dt_ln, 1)
                    if s.prev is not None:
                        eng.wait_ge(o_scale, s.prev + 1)
                        if follows(s.prev):
                            eng.wait_ge(x2_ready, s.prev)
                        for b in range(NB):
                            last = nc.scalar.activation(o_norm[:, b, :], bank_ty[:, 0, b * DM:(b + 1) * DM], ACT.Identity,
                                                        bias=shift_o[:, b:b + 1], scale=rs_o[:, b:b + 1])
                        last.then_inc(o_applied, 1)
                    if s.nxt is not None:
                        take_raw(s, 1)
                        take_raw(s, 2)
                        for g, (c0, c1) in enumerate(((0, 4), (4, 6))):
                            eng.wait_ge(conv_ready[g], s.nxt + 1)
                            nc.scalar.activation(tanh_x[:, c0:c1], half[:, c0:c1], ACT.Tanh).then_inc(tanh_x_ready[g], 1)
                        for b in range(NB):
                            eng.wait_ge(z_projected[b], s.nxt + 1)
                            if follows(s.nxt):
                                eng.wait_ge(gate_z_ready[b], s.nxt)
                            nc.scalar.activation(tanh_z[:, b, :], bank_p[:, b, :], ACT.Tanh,
                                                 scale=0.5).then_inc(tanh_z_ready[b], 1)
                    if s.prev is not None:
                        eng.wait_ge(x2_turned, s.prev + 1)
                        if follows(s.prev):
                            eng.wait_ge(logits_done, s.prev)
                        if follows(s.prev):
                            eng.wait_ge(stored_xnt, 16 * s.prev)
                        copy(x2t.rearrange("p k b t -> p (k b t)"), bank_w[:, :]).then_inc(x2t_ready, 1)
                    if s.nxt2 is not None:
                        eng.wait_ge(xnt_turned, s.nxt2 + 1)
                        if s.nxt is not None:
                            eng.wait_ge(z_projected[1], s.nxt + 1)
                        copy(xnt.rearrange("p k b t -> p (k b t)"), bank_m[:, :]).then_inc(xnt_ready, 1)
                pipeline(eng, iteration)

            @block.vector
            def _(eng):
                def tt(out, a, b, op):
                    return nc.vector.tensor_tensor(out, a, b, op)

                def stats(st, mv, sources, link, j):
                    for b in range(NB):
                        last = nc.vector.bn_stats(st[:, b, :], sources[b])
                    last.then_inc(link, 1)
                    eng.wait_ge(link, LN * j + 1)
                    eng.nop(nofuse=True)
                    for b in range(NB):
                        last = nc.vector.bn_aggr(mv[:, b, :], st[:, b, :])
                    last.then_inc(link, 1)
                    eng.wait_ge(link, LN * j + 2)

                def tap(s, k, g):
                    c0, c1 = (0, 4) if g == 0 else (4, 6)
                    if k == 0:
                        for q in (0, 1) if g == 0 else (2,):
                            eng.wait_ge(tap_ready[q], s.nxt + 1)
                    else:
                        eng.wait_ge(conv_link, TAP * s.nxt + 2 * (k - 1) + g + 1)
                    for c in range(c0, c1):
                        last = nc.vector.scalar_tensor_tensor(half[:, c], raw[:, c, :, k:k + P], conv_w[:, c, k:k + 1],
                                                              half[:, c], ALU.mult, ALU.add)
                    last.then_inc(conv_ready[g] if k == TAPS - 2 else conv_link, 1)

                def iteration(s):
                    if s.cur is not None:
                        for b in range(NB):
                            eng.wait_ge(x_tok_ready[b], s.cur + 1)
                            if follows(s.cur):
                                eng.wait_ge(intra_done[b], s.cur)
                            if follows(s.cur):
                                eng.wait_ge(xw_ready[b], s.cur)
                            tt(xdt[:, b], x_tok[:, b], sp["dt"][:, b, :].unsqueeze(2).broadcast_to([P, NH, HD]),
                               ALU.mult).then_inc(xdt_ready[b], 1)
                        eng.wait_ge(decays_ready, s.cur + 1)
                        tt(cb, bank_m[:, 0:256].rearrange("p (b t) -> p b t", b=NB),
                           upto[:, :].unsqueeze(1).broadcast_to([P, NB, P]), ALU.mult).then_inc(cb_ready, 1)
                    if s.prev2 is not None:
                        eng.wait_ge(logits_done, s.prev2 + 1)
                        if s.cur is not None:
                            eng.wait_ge(b_tok_ready, s.cur + 1)
                        if follows(s.prev2):
                            eng.wait_ge(tanh_s_done, s.prev2)
                        nc.vector.tensor_copy(logit.rearrange("p b e -> p (b e)"),
                                              bank_w[:, 0:NB * (NE + 1)]).then_inc(logit_ready, 1)
                        eng.wait_ge(logit_ready, s.prev2 + 1)
                        eng.nop(nofuse=True)
                        for b in range(NB):
                            last = nc.vector.max(top8[:, b, :], logit[:, b, 0:NE])
                        last.then_inc(route_link, 1)
                        eng.wait_ge(route_link, ROUTE * s.prev2 + 1)
                        nc.vector.tensor_scalar(neg_max, top8[:, :, 0], -1.0, None, ALU.mult).then_inc(max_ready, 1)
                        for b in range(NB):
                            last = nc.vector.match_replace(rest[:, b, :], top8[:, b, :], logit[:, b, 0:NE], NEVER)
                        last.then_inc(route_link, 1)
                        eng.wait_ge(route_link, ROUTE * s.prev2 + 2)
                        if follows(s.prev2):
                            eng.wait_ge(counts_done, s.prev2)
                        tt(chosen[:, :, :], rest, logit[:, :, 0:NE], ALU.not_equal).then_inc(chosen_ready, 1)
                    if s.cur is not None:
                        for b in range(NB):
                            eng.wait_ge(exp_ready[b], s.cur + 1)
                            if b == 0:
                                eng.wait_ge(cb_ready, s.cur + 1)
                            tt(decay[:, b], decay[:, b], cb[:, b, :].unsqueeze(1).broadcast_to([P, NH, P]),
                               ALU.mult).then_inc(mix_ready[b], 1)
                    if s.prev2 is not None:
                        eng.wait_ge(expd_ready, s.prev2 + 1)
                        eng.wait_ge(chosen_ready, s.prev2 + 1)
                        tt(picked, expd, chosen[:, :, :], ALU.mult).then_inc(route_link, 1)
                        eng.wait_ge(route_link, ROUTE * s.prev2 + 3)
                        nc.vector.tensor_reduce(top_sum, picked, AX.X, ALU.add).then_inc(route_link, 1)
                        eng.wait_ge(route_link, ROUTE * s.prev2 + 4)
                        nc.vector.reciprocal(top_inv, top_sum).then_inc(route_link, 1)
                        eng.wait_ge(route_link, ROUTE * s.prev2 + 5)
                        if follows(s.prev2):
                            eng.wait_ge(stored_weights, 32 * s.prev2)
                        tt(weights, picked, top_inv.unsqueeze(2).broadcast_to([P, NB, NE]), ALU.mult).then_inc(weights_ready, 1)
                        eng.wait_ge(counts_done, s.prev2 + 1)
                    if s.nxt is not None:
                        eng.wait_ge(dt_projected, s.nxt + 1)
                    if s.prev2 is not None:
                        if follows(s.prev2):
                            eng.wait_ge(count_kept, s.prev2)
                        nc.vector.tensor_scalar(counts[:, bass.ds(s.prev2 * P, P)], bank_w[:, 0:P], count_now[:, :], None,
                                                ALU.add).then_inc(counts_ready, 1)
                    if s.nxt is not None:
                        if follows(s.nxt):
                            eng.wait_ge(softplus, SOFT * s.nxt)
                        tt(sp["x"], bank_w[:, 256:256 + NB * NH].rearrange("p (b h) -> p b h", b=NB), dt_bias,
                           ALU.add).then_inc(dt_taken, 1)
                    if s.prev2 is not None:
                        eng.wait_ge(counts_ready, s.prev2 + 1)
                        nc.vector.tensor_copy(count_now[:, :], counts[:, bass.ds(s.prev2 * P + (P - 1), 1)]).then_inc(count_kept, 1)
                    if s.nxt is not None:
                        eng.wait_ge(dt_taken, s.nxt + 1)
                        if follows(s.nxt):
                            eng.wait_ge(dt_exp, s.nxt)
                        nc.vector.scalar_tensor_tensor(sp["nabs"], sp["x"], -1.0, sp["x"], ALU.mult, ALU.min).then_inc(softplus, 1)
                    if s.prev is not None:
                        for b in range(NB):
                            eng.wait_ge(squares_ready[b], s.prev + 1)
                        nc.vector.tensor_scalar(eps_o, square_sum, EPS / DI, 4 * EPS * EPS, ALU.mult, ALU.add)
                        eng.wait_ge(o_done, s.prev + 1)
                        stats(st_o, mv_o, [bank_ty[:, 0, b * DM:(b + 1) * DM] for b in range(NB)], o_link, s.prev)
                        tt(ve_o, mv_o[:, :, 1], eps_o, ALU.add).then_inc(o_link, 1)
                    if s.nxt2 is not None:
                        eng.wait_ge(x_loaded, 16 * s.nxt2 + 16)
                        x_now = of_step(x_all, s.nxt2)
                        stats(st_x, mv_x, [x_now[:, b, :] for b in range(NB)], ln1_link, s.nxt2)
                        if follows(s.nxt2):
                            eng.wait_ge(ln1_power, s.nxt2)
                        nc.vector.tensor_scalar(ve_x, mv_x[:, :, 1], EPS, None, ALU.add).then_inc(ln1_link, 1)
                    if s.nxt is not None:
                        eng.wait_ge(dt_exp, s.nxt + 1)
                        if follows(s.nxt):
                            eng.wait_ge(dt_ln, s.nxt)
                        nc.vector.tensor_scalar(sp["w"], sp["u"], 1.0, None, ALU.add).then_inc(softplus, 1)
                        eng.wait_ge(softplus, SOFT * s.nxt + 2)
                        nc.vector.tensor_scalar(sp["d"], sp["w"], -1.0, None, ALU.add).then_inc(softplus, 1)
                    if s.prev is not None:
                        eng.wait_ge(o_power, s.prev + 1)
                        if follows(s.prev):
                            eng.wait_ge(o_applied, s.prev)
                        nc.vector.scalar_tensor_tensor(shift_o, mv_o[:, :, 0], -1.0, rs_o, ALU.mult, ALU.mult).then_inc(o_scale, 1)
                    if s.nxt is not None:
                        eng.wait_ge(dt_ln, s.nxt + 1)
                        eng.wait_ge(softplus, SOFT * s.nxt + 3)
                        nc.vector.scalar_tensor_tensor(sp["num"], sp["d"], 0.0, sp["ln"], ALU.is_equal, ALU.add)
                        nc.vector.scalar_tensor_tensor(sp["den"], sp["d"], 0.0, sp["d"], ALU.is_equal, ALU.add).then_inc(softplus, 1)
                        eng.wait_ge(softplus, SOFT * s.nxt + 4)
                        tt(sp["q"], sp["num"], sp["u"], ALU.mult)
                        nc.vector.reciprocal(sp["inv"], sp["den"]).then_inc(softplus, 1)
                        eng.wait_ge(softplus, SOFT * s.nxt + 5)
                        tt(sp["sp"], sp["q"], sp["inv"], ALU.mult).then_inc(softplus, 1)
                        eng.wait_ge(softplus, SOFT * s.nxt + 6)
                        nc.vector.scalar_tensor_tensor(sp["dt"], sp["x"], 0.0, sp["sp"], ALU.max, ALU.add).then_inc(softplus, 1)
                        eng.wait_ge(softplus, SOFT * s.nxt + 7)
                        if s.cur is not None:
                            eng.wait_ge(seg_in_ready[1], s.cur + 1)
                            eng.wait_ge(cb_done, s.cur + 1)
                        tt(sp["a"], sp["dt"], a_neg, ALU.mult).then_inc(a_ready, 1)
                        tap(s, 0, 0)
                        tap(s, 0, 1)
                    if s.nxt2 is not None:
                        eng.wait_ge(ln1_power, s.nxt2 + 1)
                        if follows(s.nxt2):
                            eng.wait_ge(xnt_turned, s.nxt2)
                        for b in range(NB):
                            last = nc.vector.tensor_scalar(x_norm[:, b, :], x_now[:, b, :], mv_x[:, b, 0:1], rs_x[:, b:b + 1],
                                                           ALU.subtract, ALU.mult)
                        last.then_inc(x_norm_ready, 1)
                    if s.cur is not None:
                        for b in range(NB):
                            eng.wait_ge(read_done[b], s.cur + 1)
                            if s.prev is not None:
                                eng.wait_ge(y_turned[b], s.prev + 1)
                                eng.wait_ge(squares_ready[b], s.prev + 1)
                            bank = bank_m if b else bank_w
                            tt(y[:, b], bank[:, :].rearrange("p (h d) -> p h d", h=NH),
                               decays[:, 0, b, :].unsqueeze(2).broadcast_to([P, NH, HD]), ALU.mult).then_inc(inter_ready[b], 1)
                    if s.nxt is not None:
                        tap(s, 1, 0)
                        tap(s, 1, 1)
                    if s.cur is not None:
                        for b in range(NB):
                            eng.wait_ge(update_done[b], s.cur + 1)
                            eng.wait_ge(state_decayed[b], s.cur + 1)
                            tt(state[:, b], bank_p[:, b, :].rearrange("p (h d) -> p h d", h=NH), state[:, b],
                               ALU.add).then_inc(state_ready[b], 1)
                    if s.prev is not None:
                        eng.wait_ge(x2_ready, s.prev + 1)
                        x_now2 = of_step(x_all, s.prev)
                        stats(st_2, mv_2, [x_now2[:, b, :] for b in range(NB)], ln2_link, s.prev)
                        if follows(s.prev):
                            eng.wait_ge(ln2_power, s.prev)
                        nc.vector.tensor_scalar(ve_2, mv_2[:, :, 1], EPS, None, ALU.add).then_inc(ln2_link, 1)
                    if s.nxt is not None:
                        tap(s, 2, 0)
                        tap(s, 2, 1)
                    if s.cur is not None:
                        for b in range(NB):
                            eng.wait_ge(intra_done[b], s.cur + 1)
                            eng.wait_ge(inter_skip[b], s.cur + 1)
                            tt(y[:, b], bank_ty[:, b, :].rearrange("p (h d) -> p h d", h=NH), y[:, b],
                               ALU.add).then_inc(y_sum[b], 1)
                    if s.nxt is not None:
                        eng.wait_ge(conv_ready[1], s.nxt + 1)
                        nc.vector.tensor_copy(raw[:, :, :, 0:HALO], raw[:, :, :, P:P + HALO]).then_inc(halo_kept, 1)
                        if s.cur is not None:
                            eng.wait_ge(read_done[1], s.cur + 1)
                        for g, (c0, c1) in enumerate(((0, 4), (4, 6))):
                            eng.wait_ge(tanh_x_ready[g], s.nxt + 1)
                            last = nc.vector.scalar_tensor_tensor(
                                xbc[:, c0:c1].rearrange("p c b t -> p (c b t)"),
                                tanh_x[:, c0:c1].rearrange("p c b t -> p (c b t)"), 1.0,
                                half[:, c0:c1].rearrange("p c b t -> p (c b t)"), ALU.add, ALU.mult)
                        last.then_inc(xbc_ready, 1)
                    if s.prev is not None:
                        eng.wait_ge(ln2_power, s.prev + 1)
                        if follows(s.prev):
                            eng.wait_ge(x2_turned, s.prev)
                        if follows(s.prev):
                            eng.wait_ge(stored_rows, 32 * s.prev)
                        for b in range(NB):
                            last = nc.vector.tensor_scalar(x2_norm[:, b, :], x_now2[:, b, :], mv_2[:, b, 0:1], rs_2[:, b:b + 1],
                                                           ALU.subtract, ALU.mult)
                        last.then_inc(x2_norm_ready, 1)
                    if s.nxt is not None:
                        for b in range(NB):
                            eng.wait_ge(tanh_z_ready[b], s.nxt + 1)
                            if s.cur is not None:
                                eng.wait_ge(y_ready[b], s.cur + 1)
                            nc.vector.scalar_tensor_tensor(gate_z[:, b, :], tanh_z[:, b, :], 1.0, bank_p[:, b, :],
                                                           ALU.add, ALU.mult).then_inc(gate_z_ready[b], 1)
                pipeline(eng, iteration)

            @block.gpsimd
            def _(eng):
                def tt(out, a, b, op):
                    return nc.gpsimd.tensor_tensor(out, a, b, op)

                def per_head(v):
                    return v.unsqueeze(2).broadcast_to([P, NH, HD])

                def power(out, in_, link, done, j):
                    eng.wait_ge(link, LN * j + LN)
                    tt(out, in_, minus_half[:, :], ALU.pow).then_inc(done, 1)

                def iteration(s):
                    if s.cur is not None:
                        eng.wait_ge(decays_ready, s.cur + 1)
                        for b in range(NB):
                            eng.wait_ge(xdt_ready[b], s.cur + 1)
                            if follows(s.cur):
                                eng.wait_ge(update_done[b], s.cur)
                            tt(xw[:, b], xdt[:, b], per_head(decays[:, 1, b, :]), ALU.mult).then_inc(xw_ready[b], 1)
                            tt(x_tok[:, b], x_tok[:, b], per_head(d_skip), ALU.mult).then_inc(skip_ready[b], 1)
                    if s.prev is not None:
                        power(rs_o, ve_o, o_link, o_power, s.prev)
                    if s.nxt2 is not None:
                        if follows(s.nxt2):
                            eng.wait_ge(x_norm_ready, s.nxt2)
                        power(rs_x, ve_x, ln1_link, ln1_power, s.nxt2)
                    if s.prev is not None:
                        eng.wait_ge(o_applied, s.prev + 1)
                        x_now = of_step(x_all, s.prev)
                        tt(x_now, x_now, o_norm, ALU.add).then_inc(x2_ready, 1)
                    if s.cur is not None:
                        for b in range(NB):
                            eng.wait_ge(read_done[b], s.cur + 1)
                            if follows(s.cur):
                                eng.wait_ge(state_ready[b], s.cur)
                            tt(state[:, b], state[:, b], per_head(decays[:, 2, b, :]), ALU.mult).then_inc(state_decayed[b], 1)
                        for b in range(NB):
                            eng.wait_ge(inter_ready[b], s.cur + 1)
                            eng.wait_ge(skip_ready[b], s.cur + 1)
                            tt(y[:, b], y[:, b], x_tok[:, b], ALU.add).then_inc(inter_skip[b], 1)
                    if s.nxt is not None:
                        eng.wait_ge(a_ready, s.nxt + 1)
                        for b in range(NB):
                            if s.cur is not None:
                                eng.wait_ge(seg_done[b], s.cur + 1)
                            tt(seg_in[:, b], upto[:, :].unsqueeze(1).broadcast_to([P, NH, P]),
                               sp["a"][:, b, :].unsqueeze(2).broadcast_to([P, NH, P]), ALU.mult).then_inc(seg_in_ready[b], 1)
                    if s.prev is not None:
                        power(rs_2, ve_2, ln2_link, ln2_power, s.prev)
                    if s.cur is not None:
                        for b in range(NB):
                            eng.wait_ge(y_sum[b], s.cur + 1)
                            eng.wait_ge(gate_z_ready[b], s.cur + 1)
                            flat = y[:, b].rearrange("p h d -> p (h d)")
                            tt(flat, flat, gate_z[:, b, :], ALU.mult).then_inc(y_ready[b], 1)
                pipeline(eng, iteration)

        end_phase()

        memory.close()
        arena[:] = sb("experts_arena", [P, 21800]), 0
        shared = view(NB, STEPS, DM)
        wsgu_raw = shared[:, 1, 0:KD * 2 * FS // DM, :].rearrange("p (k a) d -> p k (a d)", k=KD)
        wsdown_raw = shared[:, 1, KD * 2 * FS // DM:][:, 0:FS // P, :]
        ends = view(STEPS)
        all_ends = shared[:, 0, 0:NE * TILES // DM, :].rearrange("p a (c i) -> p (a c) i", i=TILES)
        chunk_of = view(NE)
        first_of = view(NE)
        slot = view(1)
        expert = view(NE)
        past_end = view(P)
        carry = view(1)
        slot_counts = view(2, P)
        below = view(P)
        offset = view(2)
        rows = view(2, ROW)
        slot_weight = view(2)
        rows_t = view(2, KD, P)
        wgu = view(2, KD, 2 * FI)
        wdown = view(2, DM)
        tanh_e = view(2, P)
        act_e = view(2, P)
        out_e = view(2, DM)
        xt = view(KD, NB * P)
        xt_hi, xt_lo = (sb(f"xt_{part}", [P, KD, NB * P], F32R) for part in ("hi", "lo"))
        gate_s = view(NB)
        tanh_s = counts[:, 0:FS * NB].rearrange("p (c t) -> p c t", t=NB * P)
        act_s = counts[:, FS * NB:2 * FS * NB].rearrange("p (c t) -> p c t", t=NB * P)
        act_hi, act_lo = (sb(f"act_{part}", [P, FS // P, NB * P], F32R) for part in ("hi", "lo"))
        wsgu_hi, wsgu_lo = (sb(f"wsgu_{part}", [P, KD, 2 * FS], F32R) for part in ("hi", "lo"))
        wsdown_hi, wsdown_lo = (sb(f"wsdown_{part}", [P, FS // P, DM], F32R) for part in ("hi", "lo"))
        row_of = sb("row_of", [P, NE], U32)
        token_of = sb("token_of", [P, NE], U32)
        row_now = sb("row_now", [P, 2], U32)
        gather_now = sb("gather_now", [P, 2], U32)
        scatter_now = sb("scatter_now", [P, 2], U32)
        PAIRS = NE // 2
        assert PAIRS == STEPS

        carry_zero, carry_moved, counts_total, ends_kept = sem("carry_zero"), sem("carry_moved"), sem("counts_total"), sem("ends_kept")
        tables_out, ends_in, iotas, place_link, row_ready = sem("tables_out"), sem("ends_in"), sem("iotas"), sem("place_link"), sem("row_ready")
        row_copied, counts_gathered, offset_ready, token_ready = sem("row_copied"), sems("counts_gathered"), sem("offset_ready"), sem("token_ready")
        gather_copied, rows_gathered, scatter_copied, added = sem("gather_copied"), sems("rows_gathered"), sem("scatter_copied"), sem("added")
        rows_turned, rows_t_ready, weight_kept = sem("rows_turned"), sem("rows_t_ready"), sem("weight_kept")
        wgu_loaded, wdown_loaded, xt_loaded = sems("wgu_loaded"), sems("wdown_loaded"), sem("xt_loaded")
        up_e_done, tanh_e_done, act_e_half, act_e_ready, down_e_done, out_e_ready = (
            sem("up_e_done"), sem("tanh_e_done"), sem("act_e_half"), sem("act_e_ready"), sem("down_e_done"), sem("out_e_ready"))
        up_s_done, tanh_s_ready, act_s_half, act_s_ready = sems("up_s_done", 4), sems("tanh_s_ready", 4), sems("act_s_half", 4), sems("act_s_ready", 4)
        wsgu_loaded, wsdown_loaded = sem("wsgu_loaded"), sem("wsdown_loaded")
        sgu_split, sdown_split = sems("sgu_split"), sems("sdown_split")
        xt_split, act_s_full, act_hi_ready = sems("xt_split"), sems("act_s_full", 4), sems("act_hi_ready", 4)
        down_s_done, gate_s_ready, shared_ready = sem("down_s_done"), sem("gate_s_ready"), sem("shared_ready")
        counts_v = counts_d.rearrange("(i e) t -> e i t", e=NE)
        half_up = [bank_ty[:, 0, :], bank_ty[:, 1, :], bank_p[:, 0, :], bank_p[:, 1, :]]
        down_s = bank_s[:, 0, :]
        down_e = bank_s[:, 1, :]
        up_e = bank_m[:, :]
        turn_e = bank_w[:, :]

        def pairs(eng, iteration, first, last):
            lo, hi = 2, PAIRS - 2
            for q in range(first, lo):
                iteration(q, None)
            with eng.Fori(lo, hi) as q:
                iteration(q, True)
            for q in range(hi, last):
                iteration(q, None)

        def has(q, inner):
            return inner or 0 <= q < PAIRS

        with nc.Block() as block:
            @block.sync
            def _(eng):
                eng.wait_ge(carry_zero, 1)
                eng.dma_start(carry[NE:P, :], count_now[0:NE, :]).then_inc(carry_moved, 16)
                eng.wait_ge(counts_total, 1)
                for b in range(NB):
                    eng.dma_start(counts_v[:, b * STEPS:(b + 1) * STEPS, :],
                                  counts[b * NE:(b + 1) * NE, :].rearrange("e (i t) -> e i t", t=P)).then_inc(tables_out, 16)
                eng.wait_ge(iotas, 3)
                eng.dma_start(counts_v[:, TILES, :], past_end[0:NE, :]).then_inc(tables_out, 16)
                eng.wait_ge(ends_kept, 1)
                for b in range(NB):
                    eng.dma_start(ends_d[:, b * STEPS:(b + 1) * STEPS], ends[b * NE:(b + 1) * NE, :]).then_inc(tables_out, 16)
                eng.wait_ge(tables_out, 16 * 5)
                eng.dma_start(all_ends.rearrange("p e i -> p (e i)"),
                              ends_d.rearrange("e i -> (e i)").partition_broadcast(P)).then_inc(ends_in, 16)

                def iteration(q, inner):
                    if follows(q):
                        eng.wait_ge(xt_split[1], q)
                    eng.dma_start(xt.rearrange("p k t -> p (k t)"),
                                  xnt_d[bass.ds(q, 1), :, :].rearrange("o p f -> (o p) f")).then_inc(xt_loaded, 16)
                    for m in range(2):
                        if follows(q):
                            eng.wait_ge(up_e_done, q)
                        eng.dma_start(wgu[:, m], egu_d[bass.ds(2 * q + m, 1), :, :]
                                      .rearrange("o (k p) f -> p (o k) f", p=P)).then_inc(wgu_loaded[m], 16)
                    for m in range(2):
                        if follows(q):
                            eng.wait_ge(down_e_done, q)
                        eng.dma_start(wdown[:, m, :], edown_d[bass.ds(2 * q + m, 1), :, :]
                                      .rearrange("o p f -> (o p) f")).then_inc(wdown_loaded[m], 16)
                pairs(eng, iteration, 0, PAIRS)

            @block.gpsimd
            def _(eng):
                nc.gpsimd.iota(past_end, pattern=[[1, P]], base=1, channel_multiplier=0,
                               allow_small_or_imprecise_dtypes=True).then_inc(iotas, 1)
                nc.gpsimd.iota(slot, pattern=[[1, 1]], base=0, channel_multiplier=1,
                               allow_small_or_imprecise_dtypes=True).then_inc(iotas, 1)
                nc.gpsimd.iota(expert, pattern=[[1, NE]], base=0, channel_multiplier=0,
                               allow_small_or_imprecise_dtypes=True).then_inc(iotas, 1)

                def iteration(q, inner):
                    if has(q + 1, inner):
                        eng.wait_ge(token_ready, q + 2)
                        if follows(q + 1):
                            eng.wait_ge(rows_gathered[0], 16 * (q + 1))
                            eng.wait_ge(rows_gathered[1], 16 * (q + 1))
                        for m in range(2):
                            last = nc.gpsimd.tensor_copy(gather_now[:, m:m + 1], token_of[:, bass.ds(2 * q + (2 + m), 1)])
                        last.then_inc(gather_copied, 1)
                        eng.wait_ge(gather_copied, q + 2)
                        if follows(q + 1):
                            eng.wait_ge(rows_turned, q + 1)
                            eng.wait_ge(weight_kept, q + 1)
                        eng.nop(nofuse=True)
                        for m in range(2):
                            nc.gpsimd.indirect_dma_start(rows[:, m, :], None, tokens_d[:, :],
                                                         bass.IndirectOffsetOnAxis(gather_now[:, m:m + 1], 0)
                                                         ).then_inc(rows_gathered[m], 16)
                    if has(q - 1, inner):
                        if follows(q - 1):
                            eng.wait_ge(added, 32 * (q - 1))
                            eng.nop(nofuse=True)
                        for m in range(2):
                            last = nc.gpsimd.tensor_copy(scatter_now[:, m:m + 1], token_of[:, bass.ds(2 * q + (m - 2), 1)])
                        last.then_inc(scatter_copied, 1)
                        eng.wait_ge(scatter_copied, q)
                        eng.wait_ge(out_e_ready, q)
                        eng.nop(nofuse=True)
                        add(0)
                    if has(q + 2, inner):
                        if is_number(q) and q == -2:
                            eng.wait_ge(row_ready, 1)
                        if follows(q + 2):
                            eng.wait_ge(offset_ready, 2 * (q + 2))
                        for m in range(2):
                            last = nc.gpsimd.tensor_copy(row_now[:, m:m + 1], row_of[:, bass.ds(2 * q + (4 + m), 1)])
                        last.then_inc(row_copied, 1)
                        eng.wait_ge(row_copied, q + 3)
                        eng.nop(nofuse=True)
                        for m in range(2):
                            nc.gpsimd.indirect_dma_start(slot_counts[:, m, :], None, counts_d[:, :],
                                                         bass.IndirectOffsetOnAxis(row_now[:, m:m + 1], 0)
                                                         ).then_inc(counts_gathered[m], 16)
                    if has(q - 1, inner):
                        eng.wait_ge(added, 32 * (q - 1) + 16)
                        eng.nop(nofuse=True)
                        add(1)

                def add(m):
                    nc.gpsimd.indirect_dma_start(routed_d[:, :], bass.IndirectOffsetOnAxis(scatter_now[:, m:m + 1], 0),
                                                 out_e[:, m, :], None, compute_op=ALU.add).then_inc(added, 16)
                for q in (-2, -1):
                    iteration(q, None)
                pairs(eng, iteration, 0, PAIRS + 1)
                eng.wait_ge(added, 32 * PAIRS)

            @block.vector
            def _(eng):
                nc.vector.memset(carry, 0.0).then_inc(carry_zero, 1)
                eng.wait_ge(carry_moved, 16)
                nc.vector.tensor_scalar(counts[:, :], counts[:, :], carry, None, ALU.add).then_inc(counts_total, 1)
                eng.wait_ge(counts_total, 1)
                nc.vector.tensor_copy(ends, counts[:, P - 1::P]).then_inc(ends_kept, 1)
                eng.wait_ge(ends_in, 16)
                eng.wait_ge(iotas, 3)
                nc.vector.tensor_scalar(all_ends, all_ends, slot, None, ALU.is_le).then_inc(place_link, 1)
                eng.wait_ge(place_link, 1)
                nc.vector.tensor_reduce(chunk_of, all_ends, AX.X, ALU.add).then_inc(place_link, 1)
                eng.wait_ge(place_link, 2)
                nc.vector.tensor_scalar(first_of, chunk_of, float(P), None, ALU.mult)
                nc.vector.scalar_tensor_tensor(row_of[:, :], chunk_of, float(NE), expert, ALU.mult, ALU.add).then_inc(row_ready, 1)

                eng.wait_ge(sgu_split[0], 1)
                nc.vector.tensor_tensor(wsgu_lo[:, :, :], wsgu_raw, plain(wsgu_hi[:, :, :]), ALU.subtract).then_inc(sgu_split[1], 1)
                eng.wait_ge(sdown_split[0], 1)
                nc.vector.tensor_tensor(wsdown_lo[:, :, :], wsdown_raw, plain(wsdown_hi[:, :, :]), ALU.subtract).then_inc(sdown_split[1], 1)

                def activate_shared(q, c):
                    eng.wait_ge(tanh_s_ready[c], q + 1)
                    if follows(q):
                        eng.wait_ge(act_hi_ready[c], q)
                    nc.vector.scalar_tensor_tensor(act_s[:, c], tanh_s[:, c], 1.0, half_up[c][:, 0:256],
                                                   ALU.add, ALU.mult).then_inc(act_s_half[c], 1)
                    eng.wait_ge(act_s_half[c], q + 1)
                    nc.vector.tensor_tensor(act_s[:, c], act_s[:, c], half_up[c][:, 256:512],
                                            ALU.mult).then_inc(act_s_full[c], 1)

                def low_shared(q, c):
                    eng.wait_ge(act_hi_ready[c], q + 1)
                    if follows(q):
                        eng.wait_ge(down_s_done, q)
                    nc.vector.tensor_tensor(act_lo[:, c], act_s[:, c], plain(act_hi[:, c]),
                                            ALU.subtract).then_inc(act_s_ready[c], 1)

                def iteration(q, inner):
                    if has(q, inner):
                        for m in range(2):
                            eng.wait_ge(rows_gathered[m], 16 * q + 16)
                        if follows(q):
                            eng.wait_ge(out_e_ready, q)
                        for m in range(2):
                            last = nc.vector.tensor_scalar(slot_weight[:, m:m + 1],
                                                           rows[:, m, bass.ds(2 * q + (DM + m), 1)], 0.5, None, ALU.mult)
                        last.then_inc(weight_kept, 1)
                        if follows(q):
                            eng.wait_ge(shared_ready, q)
                        nc.vector.tensor_scalar(gate_s, of_step(shared_tanh, q), 1.0, 0.25, ALU.add, ALU.mult).then_inc(gate_s_ready, 1)
                        activate_shared(q, 0)
                        for c in range(1, FS // P):
                            activate_shared(q, c)
                            low_shared(q, c - 1)
                        low_shared(q, FS // P - 1)
                        eng.wait_ge(up_e_done, q + 1)
                        eng.wait_ge(tanh_e_done, q + 1)
                        if follows(q):
                            eng.wait_ge(down_e_done, q)
                        up = up_e.rearrange("p (m f j) -> p m f j", m=2, f=2)
                        nc.vector.scalar_tensor_tensor(act_e, tanh_e, 1.0, up[:, :, 0, :], ALU.add, ALU.mult).then_inc(act_e_half, 1)
                        eng.wait_ge(act_e_half, q + 1)
                        nc.vector.tensor_tensor(act_e, act_e, up[:, :, 1, :], ALU.mult).then_inc(act_e_ready, 1)
                    if has(q + 1, inner):
                        eng.wait_ge(xt_split[0], q + 2)
                        if follows(q + 1):
                            eng.wait_ge(up_s_done[3], q + 1)
                        nc.vector.tensor_tensor(xt_lo[:, :, :], xt, plain(xt_hi[:, :, :]), ALU.subtract).then_inc(xt_split[1], 1)
                    if has(q + 2, inner):
                        if follows(q + 2):
                            eng.wait_ge(token_ready, q + 2)
                        for m in range(2):
                            eng.wait_ge(counts_gathered[m], 16 * (q + 2) + 16)
                            if m:
                                eng.wait_ge(offset_ready, 2 * (q + 2) + 1)
                            nc.vector.tensor_scalar(below, slot_counts[:, m, :], slot, None, ALU.is_le, ALU.add,
                                                    accum_out=offset[:, m:m + 1]).then_inc(offset_ready, 1)
                        eng.wait_ge(offset_ready, 2 * (q + 2) + 2)
                        nc.vector.tensor_tensor(token_of[:, bass.ds(2 * q + 4, 2)], offset, first_of[:, bass.ds(2 * q + 4, 2)],
                                                ALU.add).then_inc(token_ready, 1)
                for q in (-2, -1):
                    iteration(q, None)
                pairs(eng, iteration, 0, PAIRS)

            @block.tensor
            def _(eng):
                def up_shared(q, c):
                    if follows(q):
                        eng.wait_ge(act_s_full[c], q)
                    for f in range(2):
                        columns = slice(f * FS + c * P, f * FS + (c + 1) * P)
                        parts = [(w, x, k) for k in range(KD) for w, x in ((wsgu_hi, xt_hi), (wsgu_hi, xt_lo), (wsgu_lo, xt_hi))]
                        for n, (w, x, k) in enumerate(parts):
                            last = nc.tensor.matmul(half_up[c][:, f * 256:(f + 1) * 256],
                                                    w[:, k, columns], x[:, k, :],
                                                    start=n == 0, stop=n == len(parts) - 1)
                    last.then_inc(up_s_done[c], 1)

                def iteration(q, inner):
                    if follows(q):
                        eng.wait_ge(rows_t_ready, q)
                    for m in range(2):
                        eng.wait_ge(rows_gathered[m], 16 * q + 16)
                        for k in range(KD):
                            last = nc.tensor.transpose(turn_e[:, (m * KD + k) * P:(m * KD + k + 1) * P],
                                                       rows[:, m, k * P:(k + 1) * P], identity[:, :])
                    last.then_inc(rows_turned, 1)
                    if is_number(q) and q == 0:
                        eng.wait_ge(sgu_split[1], 1)
                        eng.wait_ge(sdown_split[1], 1)
                    eng.wait_ge(xt_split[1], q + 1)
                    for c in range(FS // P):
                        up_shared(q, c)
                    eng.wait_ge(rows_t_ready, q + 1)
                    if follows(q):
                        eng.wait_ge(act_e_ready, q)
                    for m in range(2):
                        eng.wait_ge(wgu_loaded[m], 16 * q + 16)
                        for f in range(2):
                            for k in range(KD):
                                last = nc.tensor.matmul(up_e[:, (2 * m + f) * P:(2 * m + f + 1) * P],
                                                        wgu[:, m, k, f * FI:(f + 1) * FI], rows_t[:, m, k, :],
                                                        start=k == 0, stop=k == KD - 1)
                    last.then_inc(up_e_done, 1)
                    if follows(q):
                        eng.wait_ge(shared_ready, q)
                    for b in range(NB):
                        for c in range(FS // P):
                            if b == 0:
                                eng.wait_ge(act_s_ready[c], q + 1)
                            for n, (x, w) in enumerate(((act_hi, wsdown_hi), (act_hi, wsdown_lo), (act_lo, wsdown_hi))):
                                last = nc.tensor.matmul(down_s[:, b * DM:(b + 1) * DM], x[:, c, b * P:(b + 1) * P],
                                                        w[:, c, :], start=c + n == 0, stop=c == FS // P - 1 and n == 2)
                    last.then_inc(down_s_done, 1)
                    eng.wait_ge(act_e_ready, q + 1)
                    if follows(q):
                        eng.wait_ge(out_e_ready, q)
                    for m in range(2):
                        eng.wait_ge(wdown_loaded[m], 16 * q + 16)
                        last = nc.tensor.matmul(down_e[:, m * DM:(m + 1) * DM], act_e[:, m, :], wdown[:, m, :],
                                                start=True, stop=True)
                    last.then_inc(down_e_done, 1)
                pairs(eng, iteration, 0, PAIRS)

            @block.scalar
            def _(eng):
                def tanh_shared(q, c):
                    eng.wait_ge(up_s_done[c], q + 1)
                    if follows(q):
                        eng.wait_ge(act_s_half[c], q)
                    nc.scalar.activation(tanh_s[:, c], half_up[c][:, 0:256], ACT.Tanh, scale=0.5).then_inc(tanh_s_ready[c], 1)

                def high_shared(q, c):
                    eng.wait_ge(act_s_full[c], q + 1)
                    if follows(q):
                        eng.wait_ge(down_s_done, q)
                    nc.scalar.activation(act_hi[:, c], act_s[:, c], ACT.Copy).then_inc(act_hi_ready[c], 1)

                eng.dma_start(wsgu_raw, sgu_d.rearrange("(k p) f -> p k f", p=P)).then_inc(wsgu_loaded, 16)
                eng.dma_start(wsdown_raw, sdown_d.rearrange("(k p) f -> p k f", p=P)).then_inc(wsdown_loaded, 16)
                eng.wait_ge(wsgu_loaded, 16)
                nc.scalar.activation(wsgu_hi[:, :, :], wsgu_raw, ACT.Copy).then_inc(sgu_split[0], 1)
                eng.wait_ge(wsdown_loaded, 16)
                nc.scalar.activation(wsdown_hi[:, :, :], wsdown_raw, ACT.Copy).then_inc(sdown_split[0], 1)
                eng.wait_ge(tables_out, 16 * 5)

                def iteration(q, inner):
                    if has(q, inner):
                        eng.wait_ge(rows_turned, q + 1)
                        if follows(q):
                            eng.wait_ge(up_e_done, q)
                        nc.scalar.activation(rows_t.rearrange("p m k j -> p (m k j)"), turn_e, ACT.Copy).then_inc(rows_t_ready, 1)
                        tanh_shared(q, 0)
                        for c in range(1, FS // P):
                            tanh_shared(q, c)
                            high_shared(q, c - 1)
                        high_shared(q, FS // P - 1)
                        eng.wait_ge(up_e_done, q + 1)
                        if follows(q):
                            eng.wait_ge(act_e_half, q)
                        nc.scalar.activation(tanh_e, up_e.rearrange("p (m f j) -> p m f j", m=2, f=2)[:, :, 0, :], ACT.Tanh,
                                             scale=0.5).then_inc(tanh_e_done, 1)
                    if has(q + 1, inner):
                        eng.wait_ge(xt_loaded, 16 * (q + 1) + 16)
                        if follows(q + 1):
                            eng.wait_ge(up_s_done[3], q + 1)
                            eng.wait_ge(xt_split[1], q + 1)
                        nc.scalar.activation(xt_hi[:, :, :], xt, ACT.Copy).then_inc(xt_split[0], 1)
                    if has(q, inner):
                        eng.wait_ge(down_s_done, q + 1)
                        eng.wait_ge(gate_s_ready, q + 1)
                        if is_number(q) and q == 0:
                            eng.wait_ge(sgu_split[1], 1)
                            eng.wait_ge(sdown_split[1], 1)
                        for b in range(NB):
                            out = shared[:, b, q, :] if is_number(q) else shared[:, b, bass.ds(q, 1), :].rearrange("p o d -> p (o d)")
                            last = nc.scalar.activation(out, down_s[:, b * DM:(b + 1) * DM], ACT.Copy, scale=gate_s[:, b:b + 1])
                        last.then_inc(shared_ready, 1)
                        eng.wait_ge(down_e_done, q + 1)
                        eng.wait_ge(weight_kept, q + 1)
                        if follows(q):
                            eng.wait_ge(added, 32 * q)
                        for m in range(2):
                            last = nc.scalar.activation(out_e[:, m, :], down_e[:, m * DM:(m + 1) * DM], ACT.Copy,
                                                        scale=slot_weight[:, m:m + 1])
                        last.then_inc(out_e_ready, 1)
                iteration(-1, None)
                pairs(eng, iteration, 0, PAIRS)

        end_phase()

        G = 2
        GROUPS = STEPS // G
        arena[1] = NB * STEPS * DM
        routed = view(2, NB, G, DM)
        fst = view(2, NB * G, 6)
        fmv = view(2, NB * G, 2)
        fve, frs, fshift = view(2, NB * G), view(2, NB * G), view(2, NB * G)
        minus_half_g = view(NB * G)
        routed_loaded, out_stored = sems("routed_loaded"), sems("out_stored")
        f_const, f_link, f_power, f_scale, f_applied, f_ready = sem("f_const"), sem("f_link"), sem("f_power"), sem("f_scale"), sem("f_applied"), sem("f_ready")

        def groups(eng, iteration):
            iteration(0)
            with eng.Fori(1, GROUPS // 2 - 1) as i:
                iteration(i)
            iteration(GROUPS // 2 - 1)

        def rows_of(t, i, u):
            return t[:, :, bass.ds((2 * i + u) * G, G), :]

        def tokens_of(d, i, u, b):
            return d[bass.ds((2 * i + u) * (G * P) + b * LEN, G * P), :].rearrange("(s p) d -> p s d", p=P)

        with nc.Block() as block:
            @block.sync
            def _(eng):
                def load(i, u):
                    for b in range(NB):
                        eng.dma_start(routed[:, u, b], tokens_of(routed_d, i, u, b)).then_inc(routed_loaded[u], 16)

                load(0, 0)
                load(0, 1)

                def iteration(i):
                    for u in range(2):
                        eng.wait_ge(f_ready, 2 * i + u + 1)
                        for b in range(NB):
                            eng.dma_start(out_d.rearrange("b l d -> (b l) d")[bass.ds((2 * i + u) * (G * P) + b * LEN, G * P), :]
                                          .rearrange("(s p) d -> p s d", p=P),
                                          x_all[:, b, bass.ds((2 * i + u) * G, G), :]).then_inc(out_stored[u], 16)
                        if not (is_number(i) and i == GROUPS // 2 - 1):
                            load(i + 1, u)
                groups(eng, iteration)
                for u in range(2):
                    eng.wait_ge(out_stored[u], 32 * (GROUPS // 2))

            @block.vector
            def _(eng):
                nc.vector.memset(minus_half_g, -0.5).then_inc(f_const, 1)

                def iteration(i):
                    for u in range(2):
                        eng.wait_ge(routed_loaded[u], 32 * i + 32)
                        nc.vector.tensor_tensor(routed[:, u], routed[:, u], rows_of(shared, i, u), ALU.add).then_inc(f_link, 1)
                        eng.wait_ge(f_link, 8 * i + 4 * u + 1)
                        flat = routed[:, u].rearrange("p b s d -> p (b s) d")
                        for n in range(NB * G):
                            last = nc.vector.bn_stats(fst[:, u, n, :], flat[:, n, :])
                        last.then_inc(f_link, 1)
                        eng.wait_ge(f_link, 8 * i + 4 * u + 2)
                        eng.nop(nofuse=True)
                        for n in range(NB * G):
                            last = nc.vector.bn_aggr(fmv[:, u, n, :], fst[:, u, n, :])
                        last.then_inc(f_link, 1)
                        eng.wait_ge(f_link, 8 * i + 4 * u + 3)
                        nc.vector.tensor_scalar(fve[:, u, :], fmv[:, u, :, 1], EPS, None, ALU.add).then_inc(f_link, 1)
                        eng.wait_ge(f_power, 2 * i + u + 1)
                        nc.vector.scalar_tensor_tensor(fshift[:, u, :], fmv[:, u, :, 0], -1.0, frs[:, u, :],
                                                       ALU.mult, ALU.mult).then_inc(f_scale, 1)
                groups(eng, iteration)

            @block.scalar
            def _(eng):
                def iteration(i):
                    for u in range(2):
                        eng.wait_ge(f_scale, 2 * i + u + 1)
                        flat = routed[:, u].rearrange("p b s d -> p (b s) d")
                        for n in range(NB * G):
                            last = nc.scalar.activation(flat[:, n, :], flat[:, n, :], ACT.Identity,
                                                        bias=fshift[:, u, n:n + 1], scale=frs[:, u, n:n + 1])
                        last.then_inc(f_applied, 1)
                groups(eng, iteration)

            @block.gpsimd
            def _(eng):
                eng.wait_ge(f_const, 1)

                def iteration(i):
                    for u in range(2):
                        eng.wait_ge(f_link, 8 * i + 4 * u + 4)
                        nc.gpsimd.tensor_tensor(frs[:, u, :], fve[:, u, :], minus_half_g, ALU.pow).then_inc(f_power, 1)
                        eng.wait_ge(f_applied, 2 * i + u + 1)
                        nc.gpsimd.tensor_tensor(rows_of(x_all, i, u), rows_of(x_all, i, u), routed[:, u],
                                                ALU.add).then_inc(f_ready, 1)
                groups(eng, iteration)
        end_phase()


def kernel(**inputs):
    import concourse.bacc as bacc
    from concourse.bass_utils import run_bass_kernel_spmd

    a = {k: np.asarray(v) for k, v in inputs.items()}

    def by_partition(v):
        return np.moveaxis(v.reshape(-1, P, *v.shape[1:]), 1, 0)

    laid = {
        "x": a["L0_attn_X"], "w_in": a["L0_attn_W_in"].T, "conv_w": by_partition(a["L0_attn_conv_w"]), "conv_b": by_partition(a["L0_attn_conv_b"]),
        "dt_bias": a["L0_attn_dt_bias"], "a_log": a["L0_attn_A_log"], "d": a["L0_attn_D"], "norm_w": by_partition(a["L0_attn_norm_w"]),
        "w_out": a["L0_attn_W_out"].T, "gate": a["L0_ffn_gate_w"], "sgate": by_partition(a["L0_ffn_shared_gate_w"][:, 0]),
        "sgu": a["L0_ffn_shared_gate_up_w"], "sdown": a["L0_ffn_shared_down_w"],
        "egu": a["L0_ffn_expert_gate_up_w"], "edown": a["L0_ffn_expert_down_w"],
    }
    laid = {f"in_{k}": np.ascontiguousarray(v) for k, v in laid.items()}
    nc = bacc.Bacc("TRN2", target_bir_lowering=False, num_devices=1)
    args = [nc.dram_tensor(k, v.shape, mybir.dt.from_np(v.dtype), kind="ExternalInput").ap() for k, v in laid.items()]
    out = nc.dram_tensor("out_0", (NB, LEN, DM), F32, kind="ExternalOutput").ap()
    build(nc, *args, out)
    r = run_bass_kernel_spmd(nc, [laid], core_ids=[0])
    return r.results[0]["out_0"]
```

```python
import numpy as np
import concourse.bass as bass
from concourse import mybir
from concourse.alu_op_type import AluOpType as ALU
from contextlib import ExitStack

F32 = mybir.dt.float32
F32R = mybir.dt.float32r
BF16 = mybir.dt.bfloat16
U32 = mybir.dt.uint32
ACT = mybir.ActivationFunctionType
AX = mybir.AxisListType

P = 128
NB, LEN, DM = 2, 4096, 256
STEPS = LEN // P
TILES = NB * STEPS
TOK = NB * LEN
KD = DM // P
DI, NH, HD, NS = 512, 8, 64, 128
CONV = DI + 2 * NS
CT = CONV // P
TAPS = 4
HALO = TAPS - 1
KI = DI // P
EPS = 1e-5
NE, TOPK, CAP = 64, 8, 128
FI, FS = 128, 512
ROW = DM + NE
NEVER = -3.0e38


class Steps:

    def __init__(self, i, inner=False):
        def at(d):
            return i + d if inner or 0 <= i + d < STEPS else None
        self.cur, self.prev, self.prev2 = at(0), at(-1), at(-2)
        self.nxt, self.nxt2, self.far = at(1), at(2), at(5)


def is_number(j):
    return isinstance(j, int)


def plain(v):
    return v.bitcast(F32)


def follows(step):
    return not is_number(step) or step > 0


def pipeline(eng, iteration):
    first, last = 2, STEPS - 5
    for i in range(-2, first):
        iteration(Steps(i))
    with eng.Fori(first, last) as i:
        iteration(Steps(i, inner=True))
    for i in range(last, STEPS + 2):
        iteration(Steps(i))


def build(nc, x_d, w_in_d, conv_w_d, conv_b_d, dt_bias_d, a_log_d, d_d, norm_w_d, w_out_d,
          gate_d, sgate_d, sgu_d, sdown_d, egu_d, edown_d, out_d):
    tokens_d = nc.dram_tensor("token_table", (TOK + CAP, ROW), F32, kind="Internal").ap()
    routed_d = nc.dram_tensor("routed_sum", (TOK + CAP, DM), F32, kind="Internal").ap()
    counts_d = nc.dram_tensor("count_table", ((TILES + 1) * NE, P), F32, kind="Internal").ap()
    xnt_d = nc.dram_tensor("normed_transposed", (STEPS, P, KD * NB * P), F32, kind="Internal").ap()

    ctx = ExitStack()
    with ctx:
        def sb(name, shape, dt=F32):
            return ctx.enter_context(nc.sbuf_tensor(name, shape, dt))

        phase = []

        def sem(name):
            if not phase:
                phase.append(ExitStack())
            phase.append(phase[0].enter_context(nc.semaphore(name)))
            return phase[-1]

        def end_phase():
            numbers = sorted(s.num for s in phase[1:])
            starts = [n for n in numbers if n - 1 not in numbers]
            with nc.Block() as block:
                @block.sync
                def _(eng):
                    for n in starts:
                        end = n
                        while end in numbers:
                            end += 1
                        eng.sem_clear(range(n, end))
            phase.pop(0).close()
            phase.clear()

        def sems(name, n=2):
            return [sem(f"{name}{k}") for k in range(n)]

        x_all = sb("x_all", [P, NB, STEPS, DM])
        counts = sb("counts", [P, STEPS * P])
        shared_tanh = sb("shared_tanh", [P, NB, STEPS])
        identity = sb("identity", [P, P])
        upto = sb("upto", [P, P])
        beyond = sb("beyond", [P, P])
        ones = sb("ones", [P, P])
        upto_bf = sb("upto_bf", [P, P], BF16)
        count_now = sb("count_now", [P, 1])
        minus_half = sb("minus_half", [P, NB])
        bank_m = ctx.enter_context(nc.psum_tensor("bank_m", [P, 512], F32))
        bank_w = ctx.enter_context(nc.psum_tensor("bank_w", [P, 512], F32))
        bank_ty = ctx.enter_context(nc.psum_tensor("bank_ty", [P, NB, 512], F32))
        bank_p = ctx.enter_context(nc.psum_tensor("bank_p", [P, NB, 512], F32))
        bank_s = ctx.enter_context(nc.psum_tensor("bank_s", [P, 2, 512], F32))

        memory = ExitStack()
        arena = [memory.enter_context(nc.sbuf_tensor("mamba_arena", [P, 21250], F32)), 0]

        def view(*shape):
            n = int(np.prod(shape))
            v = arena[0][:, arena[1]:arena[1] + n]
            arena[1] += n
            assert arena[1] <= arena[0].shape[1], arena[1]
            names = "abcd"[:len(shape)]
            if len(shape) > 1:
                v = v.rearrange(f"p ({' '.join(names)}) -> p {' '.join(names)}",
                                **{k: s for k, s in zip(names[1:], shape[1:])})
            return v

        w_out = view(KI, DM)
        w_gate = view(KD, NE + 1)
        w_sgate = view(KD)
        conv_w = view(CT, TAPS)
        conv_b = view(CT, 1)
        norm_w = view(KI, 1)
        dt_bias = view(NB, NH)
        a_neg = view(NB, NH)
        d_skip = view(NH)
        raw = view(CT, NB, HALO + P)
        half = view(CT, NB, P)
        tanh_x = view(CT, NB, P)
        xbc = view(CT, NB, P)
        x_norm = view(NB, DM)
        setup_start = arena[1]
        tanh_z = view(NB, DI)
        gate_z = view(NB, DI)
        decay = view(NB, NH, P)
        cb = view(NB, P)
        b_tok = view(NB, NS)
        x_tok = view(NB, NH, HD)
        xdt = view(NB, NH, HD)
        xw = view(NB, NH, HD)
        y = view(NB, NH, HD)
        yt = view(NB, KI, P)
        state = view(NB, NH, HD)
        o_norm = view(NB, DM)
        x2_norm = view(NB, DM)
        x2t = view(KD, NB, P)
        weights = view(NB, NE)
        squares = o_norm.rearrange("p b d -> p (b d)")
        decays = view(3, NB, NH)
        st_x, st_o, st_2 = view(NB, 6), view(NB, 6), view(NB, 6)
        mv_x, mv_o, mv_2 = view(NB, 2), view(NB, 2), view(NB, 2)
        ve_x, ve_o, ve_2 = view(NB), view(NB), view(NB)
        rs_x, rs_o, rs_2 = view(NB), view(NB), view(NB)
        shift_o, square_sum, eps_o = view(NB), view(NB), view(NB)
        shift_x, shift_2 = view(NB), view(NB)
        sp = {k: view(NB, NH) for k in ("x", "nabs", "u", "w", "d", "ln", "num", "den", "q", "inv", "sp", "dt", "a", "a_hi", "a_lo")}
        logit = view(NB, NE + 1)
        top8 = view(NB, TOPK)
        neg_max = view(NB)
        expd = view(NB, NE)
        rest = view(NB, NE)
        picked = view(NB, NE)
        top_sum = view(NB)
        top_inv = view(NB)
        chosen = memory.enter_context(nc.sbuf_tensor("chosen", [P, NB, NE], BF16))

        def part(name, *shape):
            return memory.enter_context(nc.sbuf_tensor(name, [P, *shape], F32R))
        E_IN = 2 * DI + 2 * NS + NH
        w_in_hi, w_in_lo = part("w_in_hi", KD, E_IN), part("w_in_lo", KD, E_IN)
        xnt_hi, xnt_lo = part("xnt_hi", KD, NB, P), part("xnt_lo", KD, NB, P)
        seg_hi, seg_lo = part("seg_hi", NB, NH, P), part("seg_lo", NB, NH, P)
        beyond_r = part("beyond_r", P)
        w_in_raw = arena[0][:, setup_start:setup_start + KD * E_IN].rearrange("p (k e) -> p k e", k=KD)
        zeros = memory.enter_context(nc.sbuf_tensor("zeros", [P, ROW], F32))

        s_mem = sem("s_mem")
        s_sel = sem("s_sel")
        s_wload = sem("s_wload")
        s_wraw = sem("s_wraw")
        s_alog = sem("s_alog")
        s_prep = sem("s_prep")
        s_high = sem("s_high")

        with nc.Block() as block:
            @block.gpsimd
            def _(pool):
                for m, v in ((identity, 0.0), (upto, 1.0), (beyond, 1.0), (ones, 1.0), (minus_half, -0.5)):
                    nc.gpsimd.memset(m[:, :], v).then_inc(s_mem, 1)
                pool.wait_ge(s_mem, 5)
                nc.gpsimd.affine_select(out=identity[:, :], in_=identity[:, :], compare_op=ALU.not_equal,
                                        fill=1.0, base=0, pattern=[[-1, P]], channel_multiplier=1).then_inc(s_sel, 1)
                nc.gpsimd.affine_select(out=upto[:, :], in_=upto[:, :], compare_op=ALU.is_ge,
                                        fill=0.0, base=0, pattern=[[1, P]], channel_multiplier=-1).then_inc(s_sel, 1)
                nc.gpsimd.affine_select(out=beyond[:, :], in_=beyond[:, :], compare_op=ALU.is_gt,
                                        fill=0.0, base=0, pattern=[[-1, P]], channel_multiplier=1).then_inc(s_sel, 1)

            @block.vector
            def _(dve):
                nc.vector.memset(zeros[:, :], 0.0)
                nc.vector.memset(raw[:, :, :, 0:HALO], 0.0)
                nc.vector.memset(state, 0.0)
                nc.vector.memset(count_now[:, :], 0.0)
                dve.wait_ge(s_sel, 3)
                nc.vector.tensor_copy(upto_bf[:, :], upto[:, :])
                nc.vector.tensor_copy(beyond_r[:, :], beyond[:, :])
                dve.wait_ge(s_wraw, 16 * 8)
                nc.vector.tensor_copy(w_gate[:, :, NE], w_sgate)
                for k in range(KI):
                    nc.vector.tensor_scalar(w_out[:, k, :], w_out[:, k, :], norm_w[:, k, :], None, ALU.mult)
                nc.vector.tensor_scalar(conv_w, conv_w, 0.5, None, ALU.mult)
                nc.vector.tensor_scalar(conv_b, conv_b, 0.5, None, ALU.mult)
                dve.wait_ge(s_high, 1)
                nc.vector.tensor_tensor(w_in_lo[:, :, :], w_in_raw, plain(w_in_hi[:, :, :]), ALU.subtract)
                dve.wait_ge(s_alog, 1)
                nc.vector.tensor_scalar(a_neg, a_neg, -1.0, None, ALU.mult).then_inc(s_prep, 1)

            @block.scalar
            def _(act):
                act.wait_ge(s_wraw, 16 * 8)
                nc.scalar.activation(a_neg, a_neg, ACT.Exp).then_inc(s_alog, 1)
                act.wait_ge(s_wload, 16 * 4)
                nc.scalar.activation(w_in_hi[:, :, :], w_in_raw, ACT.Copy).then_inc(s_high, 1)

            @block.sync
            def _(sp_):
                sp_.dma_start(w_out, w_out_d.rearrange("(k p) m -> p k m", p=P)).then_inc(s_wraw, 16)
                sp_.dma_start(norm_w, norm_w_d.rearrange("p (k one) -> p k one", one=1)).then_inc(s_wraw, 16)
                sp_.dma_start(conv_w, conv_w_d).then_inc(s_wraw, 16)
                sp_.dma_start(conv_b, conv_b_d.rearrange("p (c one) -> p c one", one=1)).then_inc(s_wraw, 16)
                for b in range(NB):
                    sp_.dma_start(a_neg[:, b, :], a_log_d.partition_broadcast(P)).then_inc(s_wraw, 16)
                    sp_.dma_start(dt_bias[:, b, :], dt_bias_d.partition_broadcast(P)).then_inc(s_wload, 16)
                sp_.dma_start(d_skip, d_d.partition_broadcast(P)).then_inc(s_wraw, 16)
                sp_.dma_start(w_in_raw, w_in_d.rearrange("(k p) e -> p k e", p=P)).then_inc(s_wload, 16)
                sp_.dma_start(w_gate[:, :, 0:NE], gate_d.rearrange("(k p) e -> p k e", p=P)).then_inc(s_wload, 16)
                sp_.dma_start(w_sgate, sgate_d).then_inc(s_wraw, 16)

        def of_step(t, j):
            if is_number(j):
                return t[:, :, j]
            if len(t.shape) == 3:
                return t[:, :, bass.ds(j, 1)].rearrange("p b o -> p (b o)")
            return t[:, :, bass.ds(j, 1), :].rearrange("p b o d -> p b (o d)")

        end_phase()

        x_loaded = sem("x_loaded")
        x_norm_ready, xnt_turned, xnt_split = sem("x_norm_ready"), sem("xnt_turned"), sems("xnt_split")
        xbc_projected, raw_ready, halo_kept = sems("xbc_projected", 3), sems("raw_ready", 3), sem("halo_kept")
        tap_ready, conv_ready, tanh_x_ready = sems("tap_ready", 3), sems("conv_ready", 2), sems("tanh_x_ready", 2)
        conv_link = sem("conv_link")
        xbc_ready = sems("xbc_ready")
        z_projected, tanh_z_ready, gate_z_ready = sems("z_projected", 2), sems("tanh_z_ready", 2), sems("gate_z_ready", 2)
        dt_projected, dt_taken, dt_exp, dt_ln = sem("dt_projected"), sem("dt_taken"), sem("dt_exp"), sem("dt_ln")
        softplus = sem("softplus")
        a_ready, a_split = sem("a_ready"), sem("a_split")
        sums_done, decays_ready = sem("sums_done"), sem("decays_ready")
        cb_done, cb_ready, b_tok_ready = sem("cb_done"), sem("cb_ready"), sem("b_tok_ready")
        seg_in_ready, seg_done, exp_ready, mix_ready = sems("seg_in_ready", 2), sems("seg_done", 2), sems("exp_ready", 2), sems("mix_ready", 2)
        x_turned, x_tok_ready, xdt_ready, xw_ready = sems("x_turned", 2), sems("x_tok_ready", 2), sems("xdt_ready", 2), sems("xw_ready", 2)
        skip_ready = sems("skip_ready", 2)
        read_done, state_decayed, update_done, state_ready = sems("read_done", 2), sems("state_decayed", 2), sems("update_done", 2), sems("state_ready", 2)
        inter_ready, inter_skip, intra_done, y_sum, y_ready = sems("inter_ready", 2), sems("inter_skip", 2), sems("intra_done", 2), sems("y_sum", 2), sems("y_ready", 2)
        y_turned, yt_ready, squares_ready = sems("y_turned", 2), sems("yt_ready", 2), sems("squares_ready", 2)
        o_done, o_link, o_power, o_scale, o_applied, x2_ready = sem("o_done"), sem("o_link"), sem("o_power"), sem("o_scale"), sem("o_applied"), sem("x2_ready")
        ln1_link, ln1_power, ln1_scale, ln2_scale = sem("ln1_link"), sem("ln1_power"), sem("ln1_scale"), sem("ln2_scale")
        ln2_link, ln2_power, x2_norm_ready = sem("ln2_link"), sem("ln2_power"), sem("x2_norm_ready")
        x2_turned, x2t_ready = sem("x2_turned"), sem("x2t_ready")
        logits_done, logit_ready, max_ready, expd_ready = sem("logits_done"), sem("logit_ready"), sem("max_ready"), sem("expd_ready")
        route_link, chosen_ready, weights_ready = sem("route_link"), sem("chosen_ready"), sem("weights_ready")
        counts_done, counts_ready, count_kept, tanh_s_done = sem("counts_done"), sem("counts_ready"), sem("count_kept"), sem("tanh_s_done")
        tables_zeroed = sem("tables_zeroed")
        stored_rows, stored_xnt, stored_weights = sem("stored_rows"), sem("stored_xnt"), sem("stored_weights")

        LN, SOFT, ROUTE, TAP = 3, 7, 5, 4

        with nc.Block() as block:
            @block.sync
            def _(eng):
                def load(j):
                    eng.dma_start(of_step(x_all, j),
                                  x_d[:, bass.ds(j * P, P), :].rearrange("b p d -> p b d")).then_inc(x_loaded, 16)

                for j in range(3):
                    load(j)
                    eng.wait_ge(x_loaded, 16 * (j + 1))
                rows = (TOK + CAP) // P
                eng.dma_start(routed_d.rearrange("(p a) d -> p a d", p=P),
                              zeros[:, 0:DM].unsqueeze(1).broadcast_to([P, rows, DM])).then_inc(tables_zeroed, 16)
                eng.dma_start(tokens_d[TOK:TOK + CAP, :], zeros[:, :]).then_inc(tables_zeroed, 16)

                def iteration(s):
                    if s.far is not None:
                        load(s.far)
                        eng.wait_ge(x_loaded, 16 * s.far + 16)
                        eng.nop(nofuse=True)
                    if s.prev2 is not None:
                        eng.wait_ge(x2t_ready, s.prev2 + 1)
                        eng.nop(nofuse=True)
                        eng.dma_start(xnt_d[bass.ds(s.prev2, 1), :, :].rearrange("o p f -> (o p) f"),
                                      x2t.rearrange("p k b t -> p (k b t)")).then_inc(stored_xnt, 16)
                        eng.wait_ge(weights_ready, s.prev2 + 1)
                        eng.nop(nofuse=True)
                        for b in range(NB):
                            eng.dma_start(tokens_d[bass.ds(s.prev2 * P + b * LEN, P), DM:ROW],
                                          weights[:, b, :]).then_inc(stored_weights, 16)
                    if s.prev is not None:
                        eng.wait_ge(x2_norm_ready, s.prev + 1)
                        eng.nop(nofuse=True)
                        for b in range(NB):
                            eng.dma_start(tokens_d[bass.ds(s.prev * P + b * LEN, P), 0:DM],
                                          x2_norm[:, b, :]).then_inc(stored_rows, 16)
                pipeline(eng, iteration)
                eng.wait_ge(tables_zeroed, 32)
                eng.wait_ge(stored_rows, 32 * STEPS)
                eng.wait_ge(stored_xnt, 16 * STEPS)
                eng.wait_ge(stored_weights, 32 * STEPS)

            @block.tensor
            def _(eng):
                def transpose(out, in_):
                    return nc.tensor.transpose(out, in_, identity[:, :])

                def terms(x, w):
                    return [(n, k, x[i], w[j]) for n, (k, i, j) in
                            enumerate((k, i, j) for k in range(KD) for i, j in ((0, 0), (0, 1), (1, 0)))]

                xnt, w_in, LAST = (xnt_hi, xnt_lo), (w_in_hi, w_in_lo), 3 * KD - 1

                def seg(s, b):
                    eng.wait_ge(seg_in_ready[b], s.cur + 1)
                    for q in range(2):
                        for n, seg_in in enumerate((seg_hi, seg_lo)):
                            last = nc.tensor.matmul(bank_s[:, q, :], beyond_r[:, :],
                                                    seg_in[:, b, 4 * q:4 * q + 4, :].rearrange("p h t -> p (h t)"),
                                                    start=n == 0, stop=n == 1)
                    last.then_inc(seg_done[b], 1)

                def route(s):
                    if s.cur is not None:
                        eng.wait_ge(b_tok_ready, s.cur + 1)
                    for b in range(NB):
                        for k in range(KD):
                            last = nc.tensor.matmul(bank_w[:, b * (NE + 1):(b + 1) * (NE + 1)], x2t[:, k, b, :],
                                                    w_gate[:, k, :], start=k == 0, stop=k == KD - 1)
                    last.then_inc(logits_done, 1)

                def turn_x2(s):
                    if s.prev is not None:
                        eng.wait_ge(inter_ready[0], s.prev + 1)
                    else:
                        eng.wait_ge(counts_ready, s.prev2)
                    eng.wait_ge(x2_norm_ready, s.prev2 + 1)
                    for b in range(NB):
                        for k in range(KD):
                            last = transpose(bank_w[:, (k * NB + b) * P:(k * NB + b + 1) * P],
                                             x2_norm[:, b, k * P:(k + 1) * P])
                    last.then_inc(x2_turned, 1)

                def turn_b(s):
                    if s.prev2 is not None:
                        eng.wait_ge(x2t_ready, s.prev2 + 1)
                    elif follows(s.cur):
                        eng.wait_ge(inter_ready[0], s.cur)
                    for b in range(NB):
                        last = transpose(bank_w[:, 256 + b * P:256 + (b + 1) * P], xbc[:, 4, b, :])
                    last.then_inc(sums_done, 1)

                def project_out(s, b):
                    for c in range(KI):
                        last = nc.tensor.matmul(bank_ty[:, 0, b * DM:(b + 1) * DM], yt[:, b, c, :], w_out[:, c, :],
                                                start=c == 0, stop=c == KI - 1)
                    return last

                def project(s, g):
                    if g == 2:
                        eng.wait_ge(dt_taken, s.nxt + 1)
                        if s.cur is not None:
                            eng.wait_ge(cb_ready, s.cur + 1)
                    elif s.prev is not None:
                        eng.wait_ge(y_sum[g], s.prev + 1)
                    elif follows(s.nxt):
                        eng.wait_ge(raw_ready[g], s.nxt)
                    bank = bank_m[:, :] if g == 2 else bank_ty[:, g, :]
                    for c in (2 * g, 2 * g + 1):
                        for n, k, x, w in terms(xnt, w_in):
                            last = nc.tensor.matmul(bank[:, (c % 2) * 256:(c % 2) * 256 + 256],
                                                    w[:, k, DI + c * P:DI + (c + 1) * P],
                                                    x[:, k].rearrange("p b t -> p (b t)"),
                                                    start=n == 0, stop=n == LAST)
                    last.then_inc(xbc_projected[g], 1)

                def iteration(s):
                    if s.cur is not None:
                        if follows(s.cur):
                            eng.wait_ge(exp_ready[1], s.cur)
                        seg(s, 0)
                        eng.wait_ge(xbc_ready[0], s.cur + 1)
                        for b in range(NB):
                            eng.wait_ge(gate_z_ready[b], s.cur + 1)
                            for c in range(KI):
                                last = transpose(bank_p[:, b, c * P:(c + 1) * P], xbc[:, c, b, :])
                            last.then_inc(x_turned[b], 1)
                    if s.nxt is not None:
                        eng.wait_ge(xnt_split[1], s.nxt + 1)
                        for b in range(NB):
                            for n, k, x, w in terms(xnt, w_in):
                                last = nc.tensor.matmul(bank_m[:, 304 + b * NH:304 + (b + 1) * NH], x[:, k, b, :],
                                                        w[:, k, DI + CONV:], start=n == 0, stop=n == LAST)
                        last.then_inc(dt_projected, 1)
                    if s.cur is not None:
                        eng.wait_ge(a_ready, s.cur + 1)
                        if s.nxt is None and follows(s.cur):
                            eng.wait_ge(inter_ready[1], s.cur)
                        a2 = sp["a"].rearrange("p b h -> p (b h)")
                        for q, mask in enumerate((upto, beyond, ones)):
                            nc.tensor.matmul(bank_m[:, 256 + q * NB * NH:256 + (q + 1) * NB * NH], mask[:, :], a2,
                                             start=True, stop=True)
                        eng.wait_ge(xbc_ready[1], s.cur + 1)
                        for b in range(NB):
                            last = nc.tensor.matmul(bank_m[:, b * P:(b + 1) * P], xbc[:, 4, b, :], xbc[:, 5, b, :],
                                                    start=True, stop=True)
                        last.then_inc(cb_done, 1)
                    if s.nxt is not None:
                        project(s, 0)
                    if s.prev2 is not None:
                        turn_x2(s)
                    if s.nxt is not None:
                        project(s, 1)
                    if s.cur is not None:
                        turn_b(s)
                        eng.wait_ge(exp_ready[0], s.cur + 1)
                        seg(s, 1)
                    if s.prev2 is not None:
                        eng.wait_ge(x2t_ready, s.prev2 + 1)
                        route(s)
                    if s.nxt is not None:
                        project(s, 2)
                    if s.prev is not None:
                        for b in range(NB):
                            if s.nxt is not None:
                                eng.wait_ge(raw_ready[b], s.nxt + 1)
                            eng.wait_ge(y_ready[b], s.prev + 1)
                            for c in range(KI):
                                last = transpose(bank_ty[:, b, c * P:(c + 1) * P],
                                                 y[:, b].rearrange("p h d -> p (h d)")[:, c * P:(c + 1) * P])
                            last.then_inc(y_turned[b], 1)
                    if s.prev is not None:
                        eng.wait_ge(yt_ready[0], s.prev + 1)
                        project_out(s, 0)
                    if s.prev2 is not None:
                        eng.wait_ge(chosen_ready, s.prev2 + 1)
                        for b in range(NB):
                            last = nc.tensor.matmul(bank_w[b * NE:(b + 1) * NE, 0:P], chosen[:, b, :], upto_bf[:, :],
                                                    start=True, stop=True)
                        last.then_inc(counts_done, 1)
                    if s.prev is not None:
                        eng.wait_ge(yt_ready[1], s.prev + 1)
                        project_out(s, 1).then_inc(o_done, 1)
                    if s.cur is not None:
                        for b in range(NB):
                            if b == 0:
                                if s.prev2 is not None:
                                    eng.wait_ge(counts_ready, s.prev2 + 1)
                                eng.wait_ge(b_tok_ready, s.cur + 1)
                            else:
                                eng.wait_ge(cb_ready, s.cur + 1)
                                if s.nxt is not None:
                                    eng.wait_ge(raw_ready[2], s.nxt + 1)
                            if follows(s.cur):
                                eng.wait_ge(state_ready[b], s.cur)
                            bank = bank_m if b else bank_w
                            nc.tensor.matmul(bank[:, :], xbc[:, 5, b, :], state[:, b].rearrange("p h d -> p (h d)"),
                                             start=True, stop=True).then_inc(read_done[b], 1)
                        eng.wait_ge(b_tok_ready, s.cur + 1)
                        for b in range(NB):
                            eng.wait_ge(x_tok_ready[b], s.cur + 1)
                            eng.wait_ge(xw_ready[b], s.cur + 1)
                            nc.tensor.matmul(bank_p[:, b, :], b_tok[:, b, :], xw[:, b].rearrange("p h d -> p (h d)"),
                                             start=True, stop=True).then_inc(update_done[b], 1)
                        for b in range(NB):
                            if s.prev is not None:
                                eng.wait_ge(o_applied if b == 0 else yt_ready[1], s.prev + 1)
                            elif s.nxt is not None:
                                eng.wait_ge(raw_ready[b], s.nxt + 1)
                            eng.wait_ge(xdt_ready[b], s.cur + 1)
                            eng.wait_ge(mix_ready[b], s.cur + 1)
                            for h in range(NH):
                                last = nc.tensor.matmul(bank_ty[:, b, h * HD:(h + 1) * HD], decay[:, b, h, :],
                                                        xdt[:, b, h, :], start=True, stop=True)
                            last.then_inc(intra_done[b], 1)
                    if s.nxt2 is not None:
                        if s.cur is not None:
                            eng.wait_ge(inter_ready[1], s.cur + 1)
                        elif s.nxt is not None:
                            eng.wait_ge(raw_ready[2], s.nxt + 1)
                        eng.wait_ge(x_norm_ready, s.nxt2 + 1)
                        for b in range(NB):
                            for k in range(KD):
                                last = transpose(bank_m[:, (k * NB + b) * P:(k * NB + b + 1) * P],
                                                 x_norm[:, b, k * P:(k + 1) * P])
                        last.then_inc(xnt_turned, 1)
                    if s.nxt is not None:
                        for b in range(NB):
                            if s.cur is not None:
                                eng.wait_ge(state_ready[b], s.cur + 1)
                            for n, k, x, w in terms(xnt, w_in):
                                last = nc.tensor.matmul(bank_p[:, b, :], x[:, k, b, :], w[:, k, 0:DI],
                                                        start=n == 0, stop=n == LAST)
                            last.then_inc(z_projected[b], 1)
                pipeline(eng, iteration)

            @block.scalar
            def _(eng):
                def flat(v):
                    return v.rearrange("p h d -> p (h d)")

                def copy(out, in_):
                    return nc.scalar.activation(out, in_, ACT.Copy)

                def activate_z(s, b):
                    eng.wait_ge(z_projected[b], s.nxt + 1)
                    if follows(s.nxt):
                        eng.wait_ge(gate_z_ready[b], s.nxt)
                    nc.scalar.activation(tanh_z[:, b, :], bank_p[:, b, :], ACT.Tanh,
                                         scale=0.5).then_inc(tanh_z_ready[b], 1)

                def take_raw(s, g):
                    eng.wait_ge(xbc_projected[g], s.nxt + 1)
                    if follows(s.nxt):
                        eng.wait_ge(halo_kept, s.nxt)
                    bank = bank_m[:, :] if g == 2 else bank_ty[:, g, :]
                    copy(raw[:, 2 * g:2 * g + 2, :, HALO:], bank.rearrange("p (c b t) -> p c b t", c=2, b=NB)
                         ).then_inc(raw_ready[g], 1)

                def newest_tap(s, g):
                    eng.wait_ge(raw_ready[g], s.nxt + 1)
                    if follows(s.nxt):
                        eng.wait_ge(xbc_ready[0 if g < 2 else 1], s.nxt)
                    for c in (2 * g, 2 * g + 1):
                        last = nc.scalar.activation(half[:, c], raw[:, c, :, HALO:], ACT.Identity,
                                                    bias=conv_b[:, c, :], scale=conv_w[:, c, TAPS - 1:TAPS])
                    last.then_inc(tap_ready[g], 1)

                def take_x(s, b):
                    eng.wait_ge(x_turned[b], s.cur + 1)
                    if follows(s.cur):
                        eng.wait_ge(inter_skip[b], s.cur)
                    copy(flat(x_tok[:, b]), bank_p[:, b, :]).then_inc(x_tok_ready[b], 1)

                def decay_of(s, b):
                    eng.wait_ge(seg_done[b], s.cur + 1)
                    if follows(s.cur):
                        eng.wait_ge(intra_done[b], s.cur)
                    nc.scalar.activation(flat(decay[:, b]), bank_s[:, :, :].rearrange("p q f -> p (q f)"),
                                         ACT.Exp).then_inc(exp_ready[b], 1)

                def normalise(out, x, shift, scale):
                    for b in range(NB):
                        last = nc.scalar.activation(out[:, b, :], x[b], ACT.Identity, bias=shift[:, b:b + 1], scale=scale[:, b:b + 1])
                    return last

                def iteration(s):
                    if s.cur is not None:
                        take_x(s, 0)
                        take_x(s, 1)
                        decay_of(s, 0)
                        eng.wait_ge(cb_done, s.cur + 1)
                        if follows(s.cur):
                            eng.wait_ge(inter_ready[1], s.cur)
                            eng.wait_ge(state_decayed[1], s.cur)
                            eng.wait_ge(xw_ready[1], s.cur)
                        nc.scalar.activation(decays.rearrange("p q b h -> p (q b h)"), bank_m[:, 256:256 + 3 * NB * NH],
                                             ACT.Exp).then_inc(decays_ready, 1)
                    if s.nxt is not None:
                        eng.wait_ge(softplus, SOFT * s.nxt + 1)
                        if follows(s.nxt):
                            eng.wait_ge(a_ready, s.nxt)
                        nc.scalar.activation(sp["u"], sp["nabs"], ACT.Exp).then_inc(dt_exp, 1)
                    if s.prev2 is not None:
                        eng.wait_ge(x2_turned, s.prev2 + 1)
                        if follows(s.prev2):
                            eng.wait_ge(logits_done, s.prev2)
                            eng.wait_ge(stored_xnt, 16 * s.prev2)
                        copy(x2t.rearrange("p k b t -> p (k b t)"), bank_w[:, :]).then_inc(x2t_ready, 1)
                    if s.nxt is not None:
                        eng.wait_ge(softplus, SOFT * s.nxt + 2)
                        nc.scalar.activation(sp["ln"], sp["w"], ACT.Ln).then_inc(dt_ln, 1)
                    if s.cur is not None:
                        eng.wait_ge(sums_done, s.cur + 1)
                        if follows(s.cur):
                            eng.wait_ge(update_done[1], s.cur)
                        copy(b_tok.rearrange("p b n -> p (b n)"), bank_w[:, 256:512]).then_inc(b_tok_ready, 1)
                    if s.nxt is not None:
                        take_raw(s, 0)
                        take_raw(s, 1)
                        newest_tap(s, 0)
                        newest_tap(s, 1)
                        take_raw(s, 2)
                    if s.prev is not None:
                        for b in range(NB):
                            eng.wait_ge(y_turned[b], s.prev + 1)
                            if follows(s.prev):
                                eng.wait_ge(o_done, s.prev)
                            copy(yt[:, b].rearrange("p c t -> p (c t)"), bank_ty[:, b, :]).then_inc(yt_ready[b], 1)
                    if s.nxt is not None:
                        newest_tap(s, 2)
                    if s.prev is not None:
                        if follows(s.prev):
                            eng.wait_ge(o_link, LN * s.prev)
                            eng.wait_ge(x2_ready, s.prev)
                        for b in range(NB):
                            if b:
                                eng.wait_ge(squares_ready[0], s.prev + 1)
                            nc.scalar.activation(squares, flat(y[:, b]), ACT.Square,
                                                 accum_out=square_sum[:, b:b + 1]).then_inc(squares_ready[b], 1)
                    if s.cur is not None:
                        decay_of(s, 1)
                    if s.prev2 is not None:
                        eng.wait_ge(max_ready, s.prev2 + 1)
                        if follows(s.prev2):
                            eng.wait_ge(route_link, ROUTE * s.prev2)
                        for b in range(NB):
                            last = nc.scalar.activation(expd[:, b, :], logit[:, b, 0:NE], ACT.Exp,
                                                        bias=neg_max[:, b:b + 1])
                        last.then_inc(expd_ready, 1)
                        nc.scalar.activation(of_step(shared_tanh, s.prev2), logit[:, :, NE], ACT.Tanh,
                                             scale=0.5).then_inc(tanh_s_done, 1)
                    if s.nxt2 is not None:
                        eng.wait_ge(ln1_scale, s.nxt2 + 1)
                        if follows(s.nxt2):
                            eng.wait_ge(xnt_turned, s.nxt2)
                        x_now = of_step(x_all, s.nxt2)
                        normalise(x_norm, [x_now[:, b, :] for b in range(NB)], shift_x, rs_x).then_inc(x_norm_ready, 1)
                    if s.prev is not None:
                        eng.wait_ge(o_scale, s.prev + 1)
                        normalise(o_norm, [bank_ty[:, 0, b * DM:(b + 1) * DM] for b in range(NB)], shift_o, rs_o).then_inc(o_applied, 1)
                    if s.nxt is not None:
                        for g, (c0, c1) in enumerate(((0, 4), (4, 6))):
                            eng.wait_ge(conv_ready[g], s.nxt + 1)
                            nc.scalar.activation(tanh_x[:, c0:c1], half[:, c0:c1], ACT.Tanh).then_inc(tanh_x_ready[g], 1)
                        activate_z(s, 0)
                        activate_z(s, 1)
                    if s.nxt2 is not None:
                        eng.wait_ge(xnt_turned, s.nxt2 + 1)
                        if s.nxt is not None:
                            eng.wait_ge(z_projected[1], s.nxt + 1)
                        copy(xnt_hi[:, :, :, :].rearrange("p k b t -> p (k b t)"), bank_m[:, :]).then_inc(xnt_split[0], 1)
                    if s.prev is not None:
                        eng.wait_ge(ln2_scale, s.prev + 1)
                        if follows(s.prev):
                            eng.wait_ge(x2_turned, s.prev)
                            eng.wait_ge(stored_rows, 32 * s.prev)
                        x_now2 = of_step(x_all, s.prev)
                        normalise(x2_norm, [x_now2[:, b, :] for b in range(NB)], shift_2, rs_2).then_inc(x2_norm_ready, 1)
                pipeline(eng, iteration)

            @block.vector
            def _(eng):
                def tt(out, a, b, op):
                    return nc.vector.tensor_tensor(out, a, b, op)

                def stats(st, sources, link):
                    for b in range(NB):
                        last = nc.vector.bn_stats(st[:, b, :], sources[b])
                    last.then_inc(link, 1)

                def mean_var(st, mv, link, j):
                    eng.wait_ge(link, LN * j + 1)
                    eng.nop(nofuse=True)
                    for b in range(NB):
                        last = nc.vector.bn_aggr(mv[:, b, :], st[:, b, :])
                    last.then_inc(link, 1)

                def tap(s, k, g):
                    c0, c1 = (0, 4) if g == 0 else (4, 6)
                    if k == 0:
                        for q in (0, 1) if g == 0 else (2,):
                            eng.wait_ge(tap_ready[q], s.nxt + 1)
                    else:
                        eng.wait_ge(conv_link, TAP * s.nxt + 2 * (k - 1) + g + 1)
                    for c in range(c0, c1):
                        last = nc.vector.scalar_tensor_tensor(half[:, c], raw[:, c, :, k:k + P], conv_w[:, c, k:k + 1],
                                                              half[:, c], ALU.mult, ALU.add)
                    last.then_inc(conv_ready[g] if k == TAPS - 2 else conv_link, 1)

                def mix(s, b):
                    eng.wait_ge(exp_ready[b], s.cur + 1)
                    eng.wait_ge(cb_ready, s.cur + 1)
                    tt(decay[:, b], decay[:, b], cb[:, b, :].unsqueeze(1).broadcast_to([P, NH, P]),
                       ALU.mult).then_inc(mix_ready[b], 1)

                def iteration(s):
                    if s.cur is not None:
                        for b in range(NB):
                            eng.wait_ge(x_tok_ready[b], s.cur + 1)
                            if follows(s.cur):
                                eng.wait_ge(intra_done[b], s.cur)
                                eng.wait_ge(xw_ready[b], s.cur)
                            tt(xdt[:, b], x_tok[:, b], sp["dt"][:, b, :].unsqueeze(2).broadcast_to([P, NH, HD]),
                               ALU.mult).then_inc(xdt_ready[b], 1)
                    if s.nxt2 is not None:
                        eng.wait_ge(x_loaded, 16 * s.nxt2 + 16)
                        x_now = of_step(x_all, s.nxt2)
                        stats(st_x, [x_now[:, b, :] for b in range(NB)], ln1_link)
                    if s.nxt2 is not None:
                        mean_var(st_x, mv_x, ln1_link, s.nxt2)
                    if s.nxt2 is not None:
                        eng.wait_ge(ln1_link, LN * s.nxt2 + 2)
                        if follows(s.nxt2):
                            eng.wait_ge(ln1_power, s.nxt2)
                        nc.vector.tensor_scalar(ve_x, mv_x[:, :, 1], EPS, None, ALU.add).then_inc(ln1_link, 1)
                    if s.cur is not None:
                        eng.wait_ge(decays_ready, s.cur + 1)
                        tt(cb, bank_m[:, 0:256].rearrange("p (b t) -> p b t", b=NB),
                           upto[:, :].unsqueeze(1).broadcast_to([P, NB, P]), ALU.mult).then_inc(cb_ready, 1)
                    if s.nxt is not None:
                        eng.wait_ge(dt_projected, s.nxt + 1)
                        if follows(s.nxt):
                            eng.wait_ge(softplus, SOFT * s.nxt)
                        tt(sp["x"], bank_m[:, 304:304 + NB * NH].rearrange("p (b h) -> p b h", b=NB), dt_bias,
                           ALU.add).then_inc(dt_taken, 1)
                    if s.nxt is not None:
                        eng.wait_ge(dt_taken, s.nxt + 1)
                        if follows(s.nxt):
                            eng.wait_ge(dt_exp, s.nxt)
                        nc.vector.scalar_tensor_tensor(sp["nabs"], sp["x"], -1.0, sp["x"], ALU.mult, ALU.min).then_inc(softplus, 1)
                    if s.nxt is not None:
                        eng.wait_ge(dt_exp, s.nxt + 1)
                        if follows(s.nxt):
                            eng.wait_ge(dt_ln, s.nxt)
                        nc.vector.tensor_scalar(sp["w"], sp["u"], 1.0, None, ALU.add).then_inc(softplus, 1)
                    if s.nxt is not None:
                        eng.wait_ge(softplus, SOFT * s.nxt + 2)
                        nc.vector.tensor_scalar(sp["d"], sp["w"], -1.0, None, ALU.add).then_inc(softplus, 1)
                    if s.cur is not None:
                        mix(s, 0)
                    if s.nxt is not None:
                        eng.wait_ge(dt_ln, s.nxt + 1)
                        eng.wait_ge(softplus, SOFT * s.nxt + 3)
                        nc.vector.scalar_tensor_tensor(sp["num"], sp["d"], 0.0, sp["ln"], ALU.is_equal, ALU.add)
                        nc.vector.scalar_tensor_tensor(sp["den"], sp["d"], 0.0, sp["d"], ALU.is_equal, ALU.add).then_inc(softplus, 1)
                        eng.wait_ge(softplus, SOFT * s.nxt + 4)
                        tt(sp["q"], sp["num"], sp["u"], ALU.mult)
                        nc.vector.reciprocal(sp["inv"], sp["den"]).then_inc(softplus, 1)
                        eng.wait_ge(softplus, SOFT * s.nxt + 5)
                        tt(sp["sp"], sp["q"], sp["inv"], ALU.mult).then_inc(softplus, 1)
                    if s.nxt2 is not None:
                        eng.wait_ge(ln1_power, s.nxt2 + 1)
                        if follows(s.nxt2):
                            eng.wait_ge(x_norm_ready, s.nxt2)
                        nc.vector.scalar_tensor_tensor(shift_x, mv_x[:, :, 0], -1.0, rs_x, ALU.mult, ALU.mult).then_inc(ln1_scale, 1)
                    if s.nxt is not None:
                        eng.wait_ge(softplus, SOFT * s.nxt + 6)
                        nc.vector.scalar_tensor_tensor(sp["dt"], sp["x"], 0.0, sp["sp"], ALU.max, ALU.add).then_inc(softplus, 1)
                        eng.wait_ge(softplus, SOFT * s.nxt + 7)
                        if s.cur is not None:
                            eng.wait_ge(seg_in_ready[1], s.cur + 1)
                            eng.wait_ge(cb_done, s.cur + 1)
                        tt(sp["a"], sp["dt"], a_neg, ALU.mult).then_inc(a_ready, 1)
                        eng.wait_ge(a_ready, s.nxt + 1)
                        nc.vector.tensor_copy(sp["a_hi"].bitcast(F32R), sp["a"]).then_inc(a_split, 1)
                        eng.wait_ge(a_split, 2 * s.nxt + 1)
                        tt(sp["a_lo"], sp["a"], sp["a_hi"], ALU.subtract).then_inc(a_split, 1)
                    if s.prev2 is not None:
                        eng.wait_ge(logits_done, s.prev2 + 1)
                        if follows(s.prev2):
                            eng.wait_ge(tanh_s_done, s.prev2)
                        nc.vector.tensor_copy(logit.rearrange("p b e -> p (b e)"),
                                              bank_w[:, 0:NB * (NE + 1)]).then_inc(logit_ready, 1)
                    if s.nxt is not None:
                        tap(s, 0, 0)
                    if s.prev2 is not None:
                        eng.wait_ge(logit_ready, s.prev2 + 1)
                        eng.nop(nofuse=True)
                        for b in range(NB):
                            last = nc.vector.max(top8[:, b, :], logit[:, b, 0:NE])
                        last.then_inc(route_link, 1)
                        eng.wait_ge(route_link, ROUTE * s.prev2 + 1)
                        nc.vector.tensor_scalar(neg_max, top8[:, :, 0], -1.0, None, ALU.mult).then_inc(max_ready, 1)
                        for b in range(NB):
                            last = nc.vector.match_replace(rest[:, b, :], top8[:, b, :], logit[:, b, 0:NE], NEVER)
                        last.then_inc(route_link, 1)
                        eng.wait_ge(route_link, ROUTE * s.prev2 + 2)
                        if follows(s.prev2):
                            eng.wait_ge(counts_done, s.prev2)
                        tt(chosen[:, :, :], rest, logit[:, :, 0:NE], ALU.not_equal).then_inc(chosen_ready, 1)
                    if s.nxt is not None:
                        tap(s, 0, 1)
                    if s.prev2 is not None:
                        eng.wait_ge(counts_done, s.prev2 + 1)
                        if follows(s.prev2):
                            eng.wait_ge(count_kept, s.prev2)
                        nc.vector.tensor_scalar(counts[:, bass.ds(s.prev2 * P, P)], bank_w[:, 0:P], count_now[:, :], None,
                                                ALU.add).then_inc(counts_ready, 1)
                    if s.nxt is not None:
                        tap(s, 1, 0)
                    if s.prev is not None:
                        for b in range(NB):
                            eng.wait_ge(squares_ready[b], s.prev + 1)
                        nc.vector.tensor_scalar(eps_o, square_sum, EPS / DI, 4 * EPS * EPS, ALU.mult, ALU.add)
                    if s.prev is not None:
                        eng.wait_ge(o_done, s.prev + 1)
                        stats(st_o, [bank_ty[:, 0, b * DM:(b + 1) * DM] for b in range(NB)], o_link)
                        mean_var(st_o, mv_o, o_link, s.prev)
                        eng.wait_ge(o_link, LN * s.prev + 2)
                        tt(ve_o, mv_o[:, :, 1], eps_o, ALU.add).then_inc(o_link, 1)
                    if s.cur is not None:
                        mix(s, 1)
                    if s.prev is not None:
                        eng.wait_ge(o_power, s.prev + 1)
                        if follows(s.prev):
                            eng.wait_ge(o_applied, s.prev)
                        nc.vector.scalar_tensor_tensor(shift_o, mv_o[:, :, 0], -1.0, rs_o, ALU.mult, ALU.mult).then_inc(o_scale, 1)
                    if s.cur is not None:
                        for b in range(NB):
                            eng.wait_ge(read_done[b], s.cur + 1)
                            if s.prev is not None:
                                eng.wait_ge(y_turned[b], s.prev + 1)
                                eng.wait_ge(squares_ready[b], s.prev + 1)
                            bank = bank_m if b else bank_w
                            tt(y[:, b], bank[:, :].rearrange("p (h d) -> p h d", h=NH),
                               decays[:, 0, b, :].unsqueeze(2).broadcast_to([P, NH, HD]), ALU.mult).then_inc(inter_ready[b], 1)
                        for b in range(NB):
                            eng.wait_ge(update_done[b], s.cur + 1)
                            eng.wait_ge(state_decayed[b], s.cur + 1)
                            tt(state[:, b], bank_p[:, b, :].rearrange("p (h d) -> p h d", h=NH), state[:, b],
                               ALU.add).then_inc(state_ready[b], 1)
                    if s.prev is not None:
                        eng.wait_ge(x2_ready, s.prev + 1)
                        x_now2 = of_step(x_all, s.prev)
                        stats(st_2, [x_now2[:, b, :] for b in range(NB)], ln2_link)
                    if s.prev2 is not None:
                        eng.wait_ge(expd_ready, s.prev2 + 1)
                        eng.wait_ge(chosen_ready, s.prev2 + 1)
                        tt(picked, expd, chosen[:, :, :], ALU.mult).then_inc(route_link, 1)
                        eng.wait_ge(counts_ready, s.prev2 + 1)
                        nc.vector.tensor_copy(count_now[:, :], counts[:, bass.ds(s.prev2 * P + (P - 1), 1)]).then_inc(count_kept, 1)
                    if s.prev is not None:
                        mean_var(st_2, mv_2, ln2_link, s.prev)
                    if s.prev2 is not None:
                        eng.wait_ge(route_link, ROUTE * s.prev2 + 3)
                        nc.vector.tensor_reduce(top_sum, picked, AX.X, ALU.add).then_inc(route_link, 1)
                    if s.prev is not None:
                        eng.wait_ge(ln2_link, LN * s.prev + 2)
                        if follows(s.prev):
                            eng.wait_ge(ln2_power, s.prev)
                        nc.vector.tensor_scalar(ve_2, mv_2[:, :, 1], EPS, None, ALU.add).then_inc(ln2_link, 1)
                    if s.prev2 is not None:
                        eng.wait_ge(route_link, ROUTE * s.prev2 + 4)
                        nc.vector.reciprocal(top_inv, top_sum).then_inc(route_link, 1)
                    if s.nxt is not None:
                        tap(s, 1, 1)
                    if s.prev2 is not None:
                        eng.wait_ge(route_link, ROUTE * s.prev2 + 5)
                        if follows(s.prev2):
                            eng.wait_ge(stored_weights, 32 * s.prev2)
                        tt(weights, picked, top_inv.unsqueeze(2).broadcast_to([P, NB, NE]), ALU.mult).then_inc(weights_ready, 1)
                    if s.nxt is not None:
                        tap(s, 2, 0)
                    if s.cur is not None:
                        add_intra(s, 0)
                        add_intra(s, 1)
                    if s.prev is not None:
                        eng.wait_ge(ln2_power, s.prev + 1)
                        if follows(s.prev):
                            eng.wait_ge(x2_norm_ready, s.prev)
                        nc.vector.scalar_tensor_tensor(shift_2, mv_2[:, :, 0], -1.0, rs_2, ALU.mult, ALU.mult).then_inc(ln2_scale, 1)
                    if s.nxt is not None:
                        tap(s, 2, 1)
                        silu(s, 0)
                        gate(s, 0)
                        gate(s, 1)
                    if s.nxt2 is not None:
                        eng.wait_ge(xnt_split[0], s.nxt2 + 1)
                        tt(xnt_lo[:, :, :, :].rearrange("p k b t -> p (k b t)"), bank_m[:, :],
                           plain(xnt_hi[:, :, :, :]).rearrange("p k b t -> p (k b t)"), ALU.subtract).then_inc(xnt_split[1], 1)
                    if s.nxt is not None:
                        silu(s, 1)
                        eng.wait_ge(conv_ready[0], s.nxt + 1)
                        eng.wait_ge(conv_ready[1], s.nxt + 1)
                        nc.vector.tensor_copy(raw[:, :, :, 0:HALO], raw[:, :, :, P:P + HALO]).then_inc(halo_kept, 1)

                def silu(s, g):
                    c0, c1 = (0, 4) if g == 0 else (4, 6)
                    if s.cur is not None:
                        eng.wait_ge(read_done[1], s.cur + 1)
                    eng.wait_ge(tanh_x_ready[g], s.nxt + 1)
                    nc.vector.scalar_tensor_tensor(
                        xbc[:, c0:c1].rearrange("p c b t -> p (c b t)"),
                        tanh_x[:, c0:c1].rearrange("p c b t -> p (c b t)"), 1.0,
                        half[:, c0:c1].rearrange("p c b t -> p (c b t)"), ALU.add, ALU.mult).then_inc(xbc_ready[g], 1)

                def add_intra(s, b):
                    eng.wait_ge(intra_done[b], s.cur + 1)
                    eng.wait_ge(inter_skip[b], s.cur + 1)
                    tt(y[:, b], bank_ty[:, b, :].rearrange("p (h d) -> p h d", h=NH), y[:, b],
                       ALU.add).then_inc(y_sum[b], 1)

                def gate(s, b):
                    eng.wait_ge(tanh_z_ready[b], s.nxt + 1)
                    if s.cur is not None:
                        eng.wait_ge(y_ready[b], s.cur + 1)
                    nc.vector.scalar_tensor_tensor(gate_z[:, b, :], tanh_z[:, b, :], 1.0, bank_p[:, b, :],
                                                   ALU.add, ALU.mult).then_inc(gate_z_ready[b], 1)
                pipeline(eng, iteration)

            @block.gpsimd
            def _(eng):
                def tt(out, a, b, op):
                    return nc.gpsimd.tensor_tensor(out, a, b, op)

                def per_head(v):
                    return v.unsqueeze(2).broadcast_to([P, NH, HD])

                def power(out, in_, link, done, j):
                    eng.wait_ge(link, LN * j + LN)
                    tt(out, in_, minus_half[:, :], ALU.pow).then_inc(done, 1)

                def spread(s, j, b):
                    eng.wait_ge(a_split, 2 * j + 2)
                    if follows(j):
                        eng.wait_ge(seg_done[b], j)
                    for seg_in, a in ((seg_hi, sp["a_hi"]), (seg_lo, sp["a_lo"])):
                        last = tt(seg_in[:, b], upto[:, :].unsqueeze(1).broadcast_to([P, NH, P]),
                                  a[:, b, :].unsqueeze(2).broadcast_to([P, NH, P]), ALU.mult)
                    last.then_inc(seg_in_ready[b], 1)

                def iteration(s):
                    if s.cur is not None:
                        spread(s, s.cur, 1)
                        eng.wait_ge(decays_ready, s.cur + 1)
                        for b in range(NB):
                            eng.wait_ge(xdt_ready[b], s.cur + 1)
                            if follows(s.cur):
                                eng.wait_ge(update_done[b], s.cur)
                            tt(xw[:, b], xdt[:, b], per_head(decays[:, 1, b, :]), ALU.mult).then_inc(xw_ready[b], 1)
                            tt(x_tok[:, b], x_tok[:, b], per_head(d_skip), ALU.mult).then_inc(skip_ready[b], 1)
                    if s.nxt2 is not None:
                        if follows(s.nxt2):
                            eng.wait_ge(x_norm_ready, s.nxt2)
                        power(rs_x, ve_x, ln1_link, ln1_power, s.nxt2)
                    if s.nxt is not None:
                        spread(s, s.nxt, 0)
                    if s.prev is not None:
                        power(rs_o, ve_o, o_link, o_power, s.prev)
                    if s.cur is not None:
                        for b in range(NB):
                            eng.wait_ge(read_done[b], s.cur + 1)
                            if follows(s.cur):
                                eng.wait_ge(state_ready[b], s.cur)
                            tt(state[:, b], state[:, b], per_head(decays[:, 2, b, :]), ALU.mult).then_inc(state_decayed[b], 1)
                    if s.prev is not None:
                        eng.wait_ge(o_applied, s.prev + 1)
                        x_now = of_step(x_all, s.prev)
                        tt(x_now, x_now, o_norm, ALU.add).then_inc(x2_ready, 1)
                    if s.cur is not None:
                        for b in range(NB):
                            eng.wait_ge(inter_ready[b], s.cur + 1)
                            eng.wait_ge(skip_ready[b], s.cur + 1)
                            tt(y[:, b], y[:, b], x_tok[:, b], ALU.add).then_inc(inter_skip[b], 1)
                    if s.prev is not None:
                        if follows(s.prev):
                            eng.wait_ge(x2_norm_ready, s.prev)
                        power(rs_2, ve_2, ln2_link, ln2_power, s.prev)
                    if s.cur is not None:
                        for b in range(NB):
                            eng.wait_ge(y_sum[b], s.cur + 1)
                            eng.wait_ge(gate_z_ready[b], s.cur + 1)
                            flat = y[:, b].rearrange("p h d -> p (h d)")
                            tt(flat, flat, gate_z[:, b, :], ALU.mult).then_inc(y_ready[b], 1)
                pipeline(eng, iteration)

        end_phase()

        memory.close()
        arena[:] = sb("experts_arena", [P, 21800]), 0
        shared = view(NB, STEPS, DM)
        wsgu_raw = shared[:, 1, 0:KD * 2 * FS // DM, :].rearrange("p (k a) d -> p k (a d)", k=KD)
        wsdown_raw = shared[:, 1, KD * 2 * FS // DM:][:, 0:FS // P, :]
        ends = view(STEPS)
        ends_before = (shared[:, 0, 0:STEPS * P // (2 * DM), :].rearrange("p a d -> p (a d)").bitcast(BF16)
                       .rearrange("p (i j) -> p i j", j=P))
        carry_from = view(P)
        fold = view(NE // 2).bitcast(BF16)
        chunk_of = view(NE)
        first_of = view(NE)
        slot = view(1)
        expert = view(NE)
        past_end = view(P)
        carry = view(1)
        slot_counts = view(2, P)
        below = view(P)
        offset = view(2)
        rows = view(2, ROW)
        slot_weight = view(2)
        rows_t = view(2, KD, P)
        wgu = view(2, KD, 2 * FI)
        wdown = view(2, DM)
        tanh_e = view(2, P)
        act_e = view(2, P)
        out_e = view(2, DM)
        xt = view(KD, NB * P)
        xt_hi, xt_lo = (sb(f"xt_{part}", [P, KD, NB * P], F32R) for part in ("hi", "lo"))
        gate_s = view(NB)
        tanh_s = counts[:, 0:FS * NB].rearrange("p (c t) -> p c t", t=NB * P)
        act_s = counts[:, FS * NB:2 * FS * NB].rearrange("p (c t) -> p c t", t=NB * P)
        act_hi, act_lo = (sb(f"act_{part}", [P, FS // P, NB * P], F32R) for part in ("hi", "lo"))
        wsgu_hi, wsgu_lo = (sb(f"wsgu_{part}", [P, KD, 2 * FS], F32R) for part in ("hi", "lo"))
        wsdown_hi, wsdown_lo = (sb(f"wsdown_{part}", [P, FS // P, DM], F32R) for part in ("hi", "lo"))
        row_of = sb("row_of", [P, NE], U32)
        token_of = sb("token_of", [P, NE], U32)
        row_now = sb("row_now", [P, 2], U32)
        gather_now = sb("gather_now", [P, 2], U32)
        scatter_now = sb("scatter_now", [P, 2], U32)
        PAIRS = NE // 2
        assert PAIRS == STEPS

        carry_matrix, carry_moved, carry_ready, counts_total = sem("carry_matrix"), sem("carry_moved"), sem("carry_ready"), sem("counts_total")
        ends_kept, ends_compared, chunks_counted, chunks_kept = sem("ends_kept"), sem("ends_compared"), sem("chunks_counted"), sem("chunks_kept")
        tables_out, iotas, row_ready = sem("tables_out"), sem("iotas"), sem("row_ready")
        row_copied, counts_gathered, offset_ready, token_ready = sem("row_copied"), sems("counts_gathered"), sem("offset_ready"), sem("token_ready")
        gather_copied, rows_gathered, scatter_copied, added = sem("gather_copied"), sems("rows_gathered"), sem("scatter_copied"), sem("added")
        rows_turned, rows_t_ready, weight_kept = sem("rows_turned"), sem("rows_t_ready"), sem("weight_kept")
        wgu_loaded, wdown_loaded, xt_loaded = sems("wgu_loaded"), sems("wdown_loaded"), sem("xt_loaded")
        up_e_done, tanh_e_done, act_e_half, act_e_ready, down_e_done, out_e_ready = (
            sem("up_e_done"), sem("tanh_e_done"), sem("act_e_half"), sem("act_e_ready"), sem("down_e_done"), sem("out_e_ready"))
        up_s_done, tanh_s_ready, act_s_half, act_s_ready = sems("up_s_done", 4), sems("tanh_s_ready", 4), sems("act_s_half", 4), sems("act_s_ready", 4)
        wsgu_loaded, wsdown_loaded = sem("wsgu_loaded"), sem("wsdown_loaded")
        sgu_split, sdown_split = sems("sgu_split"), sems("sdown_split")
        xt_split, act_s_full, act_hi_ready = sems("xt_split"), sems("act_s_full", 4), sems("act_hi_ready", 4)
        down_s_done, gate_s_ready, shared_ready = sem("down_s_done"), sem("gate_s_ready"), sem("shared_ready")
        counts_v = counts_d.rearrange("(i e) t -> e i t", e=NE)
        half_up = [bank_ty[:, 0, :], bank_ty[:, 1, :], bank_p[:, 0, :], bank_p[:, 1, :]]
        down_s = bank_s[:, 0, :]
        down_e = bank_s[:, 1, :]
        up_e = bank_m[:, :]
        turn_e = bank_w[:, :]

        def pairs(eng, iteration, first, last):
            lo, hi = 2, PAIRS - 2
            for q in range(first, lo):
                iteration(q, None)
            with eng.Fori(lo, hi) as q:
                iteration(q, True)
            for q in range(hi, last):
                iteration(q, None)

        def first(q):
            return is_number(q) and q == 0

        def has(q, inner):
            return inner or 0 <= q < PAIRS

        with nc.Block() as block:
            @block.sync
            def _(eng):
                def load_xt(q):
                    eng.dma_start(xt.rearrange("p k t -> p (k t)"),
                                  xnt_d[bass.ds(q, 1), :, :].rearrange("o p f -> (o p) f")).then_inc(xt_loaded, 16)

                load_xt(0)
                eng.wait_ge(counts_total, 1)
                for b in range(NB):
                    eng.dma_start(counts_v[:, b * STEPS:(b + 1) * STEPS, :],
                                  counts[b * NE:(b + 1) * NE, :].rearrange("e (i t) -> e i t", t=P)).then_inc(tables_out, 16)
                eng.wait_ge(iotas, 3)
                eng.dma_start(counts_v[:, TILES, :], past_end[0:NE, :]).then_inc(tables_out, 16)

                def iteration(q, inner):
                    if follows(q):
                        eng.wait_ge(xt_split[1], q)
                        load_xt(q)
                    for m in range(2):
                        if follows(q):
                            eng.wait_ge(up_e_done, q)
                        eng.dma_start(wgu[:, m], egu_d[bass.ds(2 * q + m, 1), :, :]
                                      .rearrange("o (k p) f -> p (o k) f", p=P)).then_inc(wgu_loaded[m], 16)
                    for m in range(2):
                        if follows(q):
                            eng.wait_ge(down_e_done, q)
                        eng.dma_start(wdown[:, m, :], edown_d[bass.ds(2 * q + m, 1), :, :]
                                      .rearrange("o p f -> (o p) f")).then_inc(wdown_loaded[m], 16)
                pairs(eng, iteration, 0, PAIRS)

            @block.gpsimd
            def _(eng):
                nc.gpsimd.iota(past_end, pattern=[[1, P]], base=1, channel_multiplier=0,
                               allow_small_or_imprecise_dtypes=True).then_inc(iotas, 1)
                nc.gpsimd.iota(slot, pattern=[[1, 1]], base=0, channel_multiplier=1,
                               allow_small_or_imprecise_dtypes=True).then_inc(iotas, 1)
                nc.gpsimd.iota(expert, pattern=[[1, NE]], base=0, channel_multiplier=0,
                               allow_small_or_imprecise_dtypes=True).then_inc(iotas, 1)

                def iteration(q, inner):
                    if has(q + 1, inner):
                        eng.wait_ge(token_ready, q + 2)
                        if follows(q + 1):
                            eng.wait_ge(rows_gathered[0], 16 * (q + 1))
                            eng.wait_ge(rows_gathered[1], 16 * (q + 1))
                        for m in range(2):
                            last = nc.gpsimd.tensor_copy(gather_now[:, m:m + 1], token_of[:, bass.ds(2 * q + (2 + m), 1)])
                        last.then_inc(gather_copied, 1)
                        eng.wait_ge(gather_copied, q + 2)
                        if follows(q + 1):
                            eng.wait_ge(rows_turned, q + 1)
                            eng.wait_ge(weight_kept, q + 1)
                        eng.nop(nofuse=True)
                        for m in range(2):
                            nc.gpsimd.indirect_dma_start(rows[:, m, :], None, tokens_d[:, :],
                                                         bass.IndirectOffsetOnAxis(gather_now[:, m:m + 1], 0)
                                                         ).then_inc(rows_gathered[m], 16)
                    if has(q - 1, inner):
                        if follows(q - 1):
                            eng.wait_ge(added, 32 * (q - 1))
                            eng.nop(nofuse=True)
                        for m in range(2):
                            last = nc.gpsimd.tensor_copy(scatter_now[:, m:m + 1], token_of[:, bass.ds(2 * q + (m - 2), 1)])
                        last.then_inc(scatter_copied, 1)
                        eng.wait_ge(scatter_copied, q)
                        eng.wait_ge(out_e_ready, q)
                        eng.nop(nofuse=True)
                        add(0)
                    if has(q + 2, inner):
                        if is_number(q) and q == -2:
                            eng.wait_ge(row_ready, 1)
                            eng.wait_ge(tables_out, 16 * 3)
                        if follows(q + 2):
                            eng.wait_ge(offset_ready, 2 * (q + 2))
                        for m in range(2):
                            last = nc.gpsimd.tensor_copy(row_now[:, m:m + 1], row_of[:, bass.ds(2 * q + (4 + m), 1)])
                        last.then_inc(row_copied, 1)
                        eng.wait_ge(row_copied, q + 3)
                        eng.nop(nofuse=True)
                        for m in range(2):
                            nc.gpsimd.indirect_dma_start(slot_counts[:, m, :], None, counts_d[:, :],
                                                         bass.IndirectOffsetOnAxis(row_now[:, m:m + 1], 0)
                                                         ).then_inc(counts_gathered[m], 16)
                    if has(q - 1, inner):
                        eng.wait_ge(added, 32 * (q - 1) + 16)
                        eng.nop(nofuse=True)
                        add(1)

                def add(m):
                    nc.gpsimd.indirect_dma_start(routed_d[:, :], bass.IndirectOffsetOnAxis(scatter_now[:, m:m + 1], 0),
                                                 out_e[:, m, :], None, compute_op=ALU.add).then_inc(added, 16)
                for q in (-2, -1):
                    iteration(q, None)
                pairs(eng, iteration, 0, PAIRS + 1)
                eng.wait_ge(added, 32 * PAIRS)

            @block.vector
            def _(eng):
                nc.vector.memset(carry_from[:, 0:NE], 0.0)
                nc.vector.tensor_copy(carry_from[:, NE:P], identity[:, 0:NE]).then_inc(carry_matrix, 1)
                nc.vector.tensor_tensor(fold, identity[:, 0:NE], identity[:, NE:P], ALU.add)
                eng.wait_ge(carry_moved, 1)
                nc.vector.tensor_copy(carry, up_e[:, 0:1]).then_inc(carry_ready, 1)
                eng.wait_ge(carry_ready, 1)
                nc.vector.tensor_scalar(ends, counts[:, P - 1::P], carry, None, ALU.add).then_inc(ends_kept, 1)
                eng.wait_ge(ends_kept, 1)
                eng.wait_ge(iotas, 3)
                for half in range(2):
                    chunks = slice(half * STEPS // 2, (half + 1) * STEPS // 2)
                    nc.vector.tensor_tensor(ends_before[:, chunks, :], ends[:, chunks].unsqueeze(2).broadcast_to([P, STEPS // 2, P]),
                                            past_end.unsqueeze(1).broadcast_to([P, STEPS // 2, P]), ALU.is_lt
                                            ).then_inc(ends_compared, 1)
                eng.wait_ge(chunks_counted, 1)
                nc.vector.tensor_copy(chunk_of, turn_e[:, 0:NE]).then_inc(chunks_kept, 1)
                eng.wait_ge(chunks_kept, 1)
                nc.vector.tensor_scalar(first_of, chunk_of, float(P), None, ALU.mult)
                nc.vector.scalar_tensor_tensor(row_of[:, :], chunk_of, float(NE), expert, ALU.mult, ALU.add).then_inc(row_ready, 1)

                eng.wait_ge(sgu_split[0], 1)
                nc.vector.tensor_tensor(wsgu_lo[:, :, :], wsgu_raw, plain(wsgu_hi[:, :, :]), ALU.subtract).then_inc(sgu_split[1], 1)
                eng.wait_ge(sdown_split[0], 1)
                nc.vector.tensor_tensor(wsdown_lo[:, :, :], wsdown_raw, plain(wsdown_hi[:, :, :]), ALU.subtract).then_inc(sdown_split[1], 1)

                def activate_shared(q, c):
                    eng.wait_ge(tanh_s_ready[c], q + 1)
                    if follows(q):
                        eng.wait_ge(act_hi_ready[c], q)
                    nc.vector.scalar_tensor_tensor(act_s[:, c], tanh_s[:, c], 1.0, half_up[c][:, 0:256],
                                                   ALU.add, ALU.mult).then_inc(act_s_half[c], 1)
                    eng.wait_ge(act_s_half[c], q + 1)
                    nc.vector.tensor_tensor(act_s[:, c], act_s[:, c], half_up[c][:, 256:512],
                                            ALU.mult).then_inc(act_s_full[c], 1)

                def low_shared(q, c):
                    eng.wait_ge(act_hi_ready[c], q + 1)
                    if follows(q):
                        eng.wait_ge(down_s_done, q)
                    nc.vector.tensor_tensor(act_lo[:, c], act_s[:, c], plain(act_hi[:, c]),
                                            ALU.subtract).then_inc(act_s_ready[c], 1)

                def low_xt(q):
                    eng.wait_ge(xt_split[0], q + 1)
                    if follows(q):
                        eng.wait_ge(up_s_done[3], q)
                    nc.vector.tensor_tensor(xt_lo[:, :, :], xt, plain(xt_hi[:, :, :]), ALU.subtract).then_inc(xt_split[1], 1)

                def place(q):
                    if follows(q):
                        eng.wait_ge(token_ready, q)
                    for m in range(2):
                        eng.wait_ge(counts_gathered[m], 16 * q + 16)
                        if m:
                            eng.wait_ge(offset_ready, 2 * q + 1)
                        nc.vector.tensor_scalar(below, slot_counts[:, m, :], slot, None, ALU.is_le, ALU.add,
                                                accum_out=offset[:, m:m + 1]).then_inc(offset_ready, 1)
                    eng.wait_ge(offset_ready, 2 * q + 2)
                    nc.vector.tensor_tensor(token_of[:, bass.ds(2 * q, 2)], offset, first_of[:, bass.ds(2 * q, 2)],
                                            ALU.add).then_inc(token_ready, 1)

                def keep_weights(q):
                    for m in range(2):
                        eng.wait_ge(rows_gathered[m], 16 * q + 16)
                    if follows(q):
                        eng.wait_ge(out_e_ready, q)
                    for m in range(2):
                        last = nc.vector.tensor_scalar(slot_weight[:, m:m + 1],
                                                       rows[:, m, bass.ds(2 * q + (DM + m), 1)], 0.5, None, ALU.mult)
                    last.then_inc(weight_kept, 1)

                def iteration(q, inner):
                    if has(q, inner):
                        if not first(q):
                            keep_weights(q)
                        if follows(q):
                            eng.wait_ge(shared_ready, q)
                        nc.vector.tensor_scalar(gate_s, of_step(shared_tanh, q), 1.0, 0.25, ALU.add, ALU.mult).then_inc(gate_s_ready, 1)
                        activate_shared(q, 0)
                        for c in range(1, FS // P):
                            activate_shared(q, c)
                            low_shared(q, c - 1)
                        low_shared(q, FS // P - 1)
                        if first(q):
                            place(1)
                            keep_weights(q)
                        eng.wait_ge(up_e_done, q + 1)
                        eng.wait_ge(tanh_e_done, q + 1)
                        if follows(q):
                            eng.wait_ge(down_e_done, q)
                        up = up_e.rearrange("p (m f j) -> p m f j", m=2, f=2)
                        nc.vector.scalar_tensor_tensor(act_e, tanh_e, 1.0, up[:, :, 0, :], ALU.add, ALU.mult).then_inc(act_e_half, 1)
                        eng.wait_ge(act_e_half, q + 1)
                        nc.vector.tensor_tensor(act_e, act_e, up[:, :, 1, :], ALU.mult).then_inc(act_e_ready, 1)
                    if has(q + 1, inner) and not first(q + 1):
                        low_xt(q + 1)
                    if has(q + 2, inner) and not first(q + 1):
                        place(q + 2)
                low_xt(0)
                for q in (-2, -1):
                    iteration(q, None)
                pairs(eng, iteration, 0, PAIRS)

            @block.tensor
            def _(eng):
                def up_shared(q, c):
                    if follows(q):
                        eng.wait_ge(act_s_full[c], q)
                    for f in range(2):
                        columns = slice(f * FS + c * P, f * FS + (c + 1) * P)
                        parts = [(w, x, k) for k in range(KD) for w, x in ((wsgu_hi, xt_hi), (wsgu_hi, xt_lo), (wsgu_lo, xt_hi))]
                        for n, (w, x, k) in enumerate(parts):
                            last = nc.tensor.matmul(half_up[c][:, f * 256:(f + 1) * 256],
                                                    w[:, k, columns], x[:, k, :],
                                                    start=n == 0, stop=n == len(parts) - 1)
                    last.then_inc(up_s_done[c], 1)

                def turn_rows(q):
                    if follows(q):
                        eng.wait_ge(rows_t_ready, q)
                    for m in range(2):
                        eng.wait_ge(rows_gathered[m], 16 * q + 16)
                        for k in range(KD):
                            last = nc.tensor.transpose(turn_e[:, (m * KD + k) * P:(m * KD + k + 1) * P],
                                                       rows[:, m, k * P:(k + 1) * P], identity[:, :])
                    last.then_inc(rows_turned, 1)

                def iteration(q, inner):
                    if not first(q):
                        turn_rows(q)
                    if is_number(q) and q == 0:
                        eng.wait_ge(sgu_split[1], 1)
                        eng.wait_ge(sdown_split[1], 1)
                    eng.wait_ge(xt_split[1], q + 1)
                    for c in range(FS // P):
                        up_shared(q, c)
                    if first(q):
                        turn_rows(q)
                    eng.wait_ge(rows_t_ready, q + 1)
                    if follows(q):
                        eng.wait_ge(act_e_ready, q)
                    for m in range(2):
                        eng.wait_ge(wgu_loaded[m], 16 * q + 16)
                        for f in range(2):
                            for k in range(KD):
                                last = nc.tensor.matmul(up_e[:, (2 * m + f) * P:(2 * m + f + 1) * P],
                                                        wgu[:, m, k, f * FI:(f + 1) * FI], rows_t[:, m, k, :],
                                                        start=k == 0, stop=k == KD - 1)
                    last.then_inc(up_e_done, 1)
                    if follows(q):
                        eng.wait_ge(shared_ready, q)
                    for b in range(NB):
                        for c in range(FS // P):
                            if b == 0:
                                eng.wait_ge(act_s_ready[c], q + 1)
                            for n, (x, w) in enumerate(((act_hi, wsdown_hi), (act_hi, wsdown_lo), (act_lo, wsdown_hi))):
                                last = nc.tensor.matmul(down_s[:, b * DM:(b + 1) * DM], x[:, c, b * P:(b + 1) * P],
                                                        w[:, c, :], start=c + n == 0, stop=c == FS // P - 1 and n == 2)
                    last.then_inc(down_s_done, 1)
                    eng.wait_ge(act_e_ready, q + 1)
                    if follows(q):
                        eng.wait_ge(out_e_ready, q)
                    for m in range(2):
                        eng.wait_ge(wdown_loaded[m], 16 * q + 16)
                        last = nc.tensor.matmul(down_e[:, m * DM:(m + 1) * DM], act_e[:, m, :], wdown[:, m, :],
                                                start=True, stop=True)
                    last.then_inc(down_e_done, 1)
                eng.wait_ge(carry_matrix, 1)
                nc.tensor.matmul(up_e[:, 0:1], carry_from, count_now[:, :], start=True, stop=True).then_inc(carry_moved, 1)
                for i in range(STEPS):
                    if i in (0, STEPS // 2):
                        eng.wait_ge(ends_compared, 1 if i == 0 else 2)
                    last = nc.tensor.matmul(turn_e[:, 0:NE], ends_before[:, i, :], fold, start=i == 0, stop=i == STEPS - 1)
                last.then_inc(chunks_counted, 1)
                pairs(eng, iteration, 0, PAIRS)

            @block.scalar
            def _(eng):
                def tanh_shared(q, c):
                    eng.wait_ge(up_s_done[c], q + 1)
                    if follows(q):
                        eng.wait_ge(act_s_half[c], q)
                    nc.scalar.activation(tanh_s[:, c], half_up[c][:, 0:256], ACT.Tanh, scale=0.5).then_inc(tanh_s_ready[c], 1)

                def high_shared(q, c):
                    eng.wait_ge(act_s_full[c], q + 1)
                    if follows(q):
                        eng.wait_ge(down_s_done, q)
                    nc.scalar.activation(act_hi[:, c], act_s[:, c], ACT.Copy).then_inc(act_hi_ready[c], 1)

                eng.dma_start(wsgu_raw, sgu_d.rearrange("(k p) f -> p k f", p=P)).then_inc(wsgu_loaded, 16)
                eng.dma_start(wsdown_raw, sdown_d.rearrange("(k p) f -> p k f", p=P)).then_inc(wsdown_loaded, 16)
                eng.wait_ge(carry_ready, 1)
                eng.wait_ge(ends_kept, 1)
                nc.scalar.activation(counts[:, :], counts[:, :], ACT.Identity, bias=carry).then_inc(counts_total, 1)
                eng.wait_ge(wsgu_loaded, 16)
                nc.scalar.activation(wsgu_hi[:, :, :], wsgu_raw, ACT.Copy).then_inc(sgu_split[0], 1)
                eng.wait_ge(wsdown_loaded, 16)
                nc.scalar.activation(wsdown_hi[:, :, :], wsdown_raw, ACT.Copy).then_inc(sdown_split[0], 1)

                def take_rows(q):
                    eng.wait_ge(rows_turned, q + 1)
                    if follows(q):
                        eng.wait_ge(up_e_done, q)
                    nc.scalar.activation(rows_t.rearrange("p m k j -> p (m k j)"), turn_e, ACT.Copy).then_inc(rows_t_ready, 1)

                def iteration(q, inner):
                    if has(q, inner):
                        if first(q):
                            eng.wait_ge(tables_out, 16 * 3)
                        else:
                            take_rows(q)
                        tanh_shared(q, 0)
                        for c in range(1, FS // P):
                            tanh_shared(q, c)
                            high_shared(q, c - 1)
                        high_shared(q, FS // P - 1)
                        if first(q):
                            take_rows(q)
                        eng.wait_ge(up_e_done, q + 1)
                        if follows(q):
                            eng.wait_ge(act_e_half, q)
                        nc.scalar.activation(tanh_e, up_e.rearrange("p (m f j) -> p m f j", m=2, f=2)[:, :, 0, :], ACT.Tanh,
                                             scale=0.5).then_inc(tanh_e_done, 1)
                    if has(q + 1, inner):
                        eng.wait_ge(xt_loaded, 16 * (q + 1) + 16)
                        if follows(q + 1):
                            eng.wait_ge(up_s_done[3], q + 1)
                            eng.wait_ge(xt_split[1], q + 1)
                        nc.scalar.activation(xt_hi[:, :, :], xt, ACT.Copy).then_inc(xt_split[0], 1)
                    if has(q, inner):
                        eng.wait_ge(down_s_done, q + 1)
                        eng.wait_ge(gate_s_ready, q + 1)
                        if is_number(q) and q == 0:
                            eng.wait_ge(sgu_split[1], 1)
                            eng.wait_ge(sdown_split[1], 1)
                        for b in range(NB):
                            out = shared[:, b, q, :] if is_number(q) else shared[:, b, bass.ds(q, 1), :].rearrange("p o d -> p (o d)")
                            last = nc.scalar.activation(out, down_s[:, b * DM:(b + 1) * DM], ACT.Copy, scale=gate_s[:, b:b + 1])
                        last.then_inc(shared_ready, 1)
                        eng.wait_ge(down_e_done, q + 1)
                        eng.wait_ge(weight_kept, q + 1)
                        if follows(q):
                            eng.wait_ge(added, 32 * q)
                        for m in range(2):
                            last = nc.scalar.activation(out_e[:, m, :], down_e[:, m * DM:(m + 1) * DM], ACT.Copy,
                                                        scale=slot_weight[:, m:m + 1])
                        last.then_inc(out_e_ready, 1)
                iteration(-1, None)
                pairs(eng, iteration, 0, PAIRS)

        end_phase()

        G = 1
        GROUPS = STEPS // G
        DEPTH = 8
        ROUNDS = GROUPS // DEPTH
        arena[1] = NB * STEPS * DM
        routed = view(DEPTH, NB, G, DM)
        fst = view(DEPTH, NB * G, 6)
        fmv = view(DEPTH, NB * G, 2)
        fve, frs, fshift = view(DEPTH, NB * G), view(DEPTH, NB * G), view(DEPTH, NB * G)
        minus_half_g = view(NB * G)
        routed_loaded, out_stored = sems("routed_loaded", DEPTH), sems("out_stored", DEPTH)
        f_added, f_stats, f_mean, f_var = sem("f_added"), sem("f_stats"), sem("f_mean"), sem("f_var")
        f_const, f_power, f_scale, f_applied, f_ready = sem("f_const"), sem("f_power"), sem("f_scale"), sem("f_applied"), sem("f_ready")

        def rounds(eng, stages):
            def one(i):
                for u in range(DEPTH):
                    for stage, behind in stages:
                        if not (is_number(i) and i * DEPTH + u < behind):
                            stage(i * DEPTH + (u - behind), i + (u - behind) // DEPTH, (u - behind) % DEPTH)
            one(0)
            with eng.Fori(1, ROUNDS - 1) as i:
                one(i)
            one(ROUNDS - 1)
            for g in range(GROUPS, GROUPS + max(behind for _, behind in stages)):
                for stage, behind in stages:
                    if g - behind < GROUPS:
                        stage(g - behind, (g - behind) // DEPTH, (g - behind) % DEPTH)

        def rows_of(t, g):
            return t[:, :, bass.ds(g * G, G), :]

        def tokens_of(d, g):
            return d.rearrange("(b l) d -> b l d", b=NB)[:, bass.ds(g * P, P), :].rearrange("b p d -> p b d")

        with nc.Block() as block:
            @block.sync
            def _(eng):
                out_rows = out_d.rearrange("b l d -> (b l) d")

                def load(g, u):
                    eng.dma_start(routed[:, u, :, 0, :], tokens_of(routed_d[0:TOK, :], g)).then_inc(routed_loaded[u], 16)

                def store(g, r, u):
                    eng.wait_ge(f_ready, g + 1)
                    eng.dma_start(tokens_of(out_rows, g), x_all[:, :, bass.ds(g, 1), :].rearrange("p b s d -> p (b s) d")).then_inc(out_stored[u], 16)
                    if not (is_number(r) and r == ROUNDS - 1):
                        load(g + DEPTH, u)

                for u in range(DEPTH):
                    load(u, u)
                rounds(eng, [(store, 0)])
                for u in range(DEPTH):
                    eng.wait_ge(out_stored[u], 16 * ROUNDS)

            @block.vector
            def _(eng):
                nc.vector.memset(minus_half_g, -0.5).then_inc(f_const, 1)

                def rows_flat(u):
                    return routed[:, u].rearrange("p b s d -> p (b s) d")

                def add_shared(g, r, u):
                    eng.wait_ge(routed_loaded[u], 16 * r + 16)
                    nc.vector.tensor_tensor(routed[:, u], routed[:, u], rows_of(shared, g), ALU.add).then_inc(f_added, 1)

                def measure(g, r, u):
                    eng.wait_ge(f_added, g + 1)
                    for n in range(NB * G):
                        last = nc.vector.bn_stats(fst[:, u, n, :], rows_flat(u)[:, n, :])
                    last.then_inc(f_stats, 1)

                def aggregate(g, r, u):
                    eng.wait_ge(f_stats, g + 1)
                    eng.nop(nofuse=True)
                    for n in range(NB * G):
                        last = nc.vector.bn_aggr(fmv[:, u, n, :], fst[:, u, n, :])
                    last.then_inc(f_mean, 1)

                def add_eps(g, r, u):
                    eng.wait_ge(f_mean, g + 1)
                    nc.vector.tensor_scalar(fve[:, u, :], fmv[:, u, :, 1], EPS, None, ALU.add).then_inc(f_var, 1)

                def shift(g, r, u):
                    eng.wait_ge(f_power, g + 1)
                    nc.vector.scalar_tensor_tensor(fshift[:, u, :], fmv[:, u, :, 0], -1.0, frs[:, u, :],
                                                   ALU.mult, ALU.mult).then_inc(f_scale, 1)
                rounds(eng, [(add_shared, 0), (aggregate, 1), (measure, 0), (add_eps, 1), (shift, 2)])

            @block.scalar
            def _(eng):
                def normalise(g, r, u):
                    eng.wait_ge(f_scale, g + 1)
                    flat = routed[:, u].rearrange("p b s d -> p (b s) d")
                    for n in range(NB * G):
                        last = nc.scalar.activation(flat[:, n, :], flat[:, n, :], ACT.Identity,
                                                    bias=fshift[:, u, n:n + 1], scale=frs[:, u, n:n + 1])
                    last.then_inc(f_applied, 1)
                rounds(eng, [(normalise, 0)])

            @block.gpsimd
            def _(eng):
                eng.wait_ge(f_const, 1)

                def power(g, r, u):
                    eng.wait_ge(f_var, g + 1)
                    nc.gpsimd.tensor_tensor(frs[:, u, :], fve[:, u, :], minus_half_g, ALU.pow).then_inc(f_power, 1)

                def add_residual(g, r, u):
                    eng.wait_ge(f_applied, g + 1)
                    nc.gpsimd.tensor_tensor(rows_of(x_all, g), rows_of(x_all, g), routed[:, u],
                                            ALU.add).then_inc(f_ready, 1)
                rounds(eng, [(power, 0), (add_residual, 1)])
        end_phase()


def kernel(**inputs):
    import concourse.bacc as bacc
    from concourse.bass_utils import run_bass_kernel_spmd

    a = {k: np.asarray(v) for k, v in inputs.items()}

    def by_partition(v):
        return np.moveaxis(v.reshape(-1, P, *v.shape[1:]), 1, 0)

    laid = {
        "x": a["L0_attn_X"], "w_in": a["L0_attn_W_in"].T, "conv_w": by_partition(a["L0_attn_conv_w"]), "conv_b": by_partition(a["L0_attn_conv_b"]),
        "dt_bias": a["L0_attn_dt_bias"], "a_log": a["L0_attn_A_log"], "d": a["L0_attn_D"], "norm_w": by_partition(a["L0_attn_norm_w"]),
        "w_out": a["L0_attn_W_out"].T, "gate": a["L0_ffn_gate_w"], "sgate": by_partition(a["L0_ffn_shared_gate_w"][:, 0]),
        "sgu": a["L0_ffn_shared_gate_up_w"], "sdown": a["L0_ffn_shared_down_w"],
        "egu": a["L0_ffn_expert_gate_up_w"], "edown": a["L0_ffn_expert_down_w"],
    }
    laid = {f"in_{k}": np.ascontiguousarray(v) for k, v in laid.items()}
    nc = bacc.Bacc("TRN2", target_bir_lowering=False, num_devices=1)
    args = [nc.dram_tensor(k, v.shape, mybir.dt.from_np(v.dtype), kind="ExternalInput").ap() for k, v in laid.items()]
    out = nc.dram_tensor("out_0", (NB, LEN, DM), F32, kind="ExternalOutput").ap()
    build(nc, *args, out)
    r = run_bass_kernel_spmd(nc, [laid], core_ids=[0])
    return r.results[0]["out_0"]
```
